# Optimizing a Trainium2 kernel written in Bass

```python
import numpy as np
import jax
import jax.numpy as jnp

def _softmax(x, axis=-1):
    return jax.nn.softmax(x, axis=axis)

def _gelu(x):
    return jax.nn.gelu(x, approximate=True)

def _silu(x):
    return jax.nn.silu(x)

def _sigmoid(x):
    return jax.nn.sigmoid(x)

def _layernorm(x, axis=-1, eps=1e-05):
    m = jnp.mean(x, axis=axis, keepdims=True)
    v = jnp.var(x, axis=axis, keepdims=True)
    return (x - m) / jnp.sqrt(v + eps)

def _scatter_add(tgt, idx, src, axis=0):
    return tgt.at[idx].add(src)

def _segment_sum(src, seg, n):
    return jax.ops.segment_sum(src, seg, n)
kernel_name = 'mk_macaron_d1_jaxref_r4_3b55d4'

def setup_inputs(seed: int=0):
    np.random.seed(seed)
    _w = jnp.asarray

    def _L0_attn_setup():
        import jax, jax.numpy as jnp
        import numpy as np
        import math
        B, T, C = (2, 512, 256)
        H, L = (16, 64)
        DH = C // H
        DHE = DH // 2
        THETA = 10000.0

        def _rope_cache(t, dim):
            inv_freq = 1.0 / THETA ** (jnp.arange(0, dim, 2, dtype=jnp.float32) / dim)
            freqs = jnp.arange(t, dtype=jnp.float32)[:, None] * inv_freq[None, :]
            emb = jnp.concatenate((freqs, freqs), axis=-1)
            return (jnp.cos(emb), jnp.sin(emb))

        def _apply_rope(x, cos, sin):
            x1 = x[..., 0::2]
            x2 = x[..., 1::2]
            rot = jnp.stack((-x2, x1), axis=-1).reshape(x.shape)
            return x * cos[None, None] + rot * sin[None, None]
        key = jax.random.key(seed)
        ks = jax.random.split(key, 10)
        s = 0.02
        return {'x': jax.random.normal(ks[0], (B, T, C), jnp.float32), 'Wq_down': jax.random.normal(ks[1], (C, H * L), jnp.float32) * s, 'Wk_down': jax.random.normal(ks[2], (C, H * L), jnp.float32) * s, 'Wv_down': jax.random.normal(ks[3], (C, H * L), jnp.float32) * s, 'Wq_up_c': jax.random.normal(ks[4], (L, DHE), jnp.float32) * s, 'Wq_up_e': jax.random.normal(ks[5], (L, DHE), jnp.float32) * s, 'Wk_up_c': jax.random.normal(ks[6], (L, DHE), jnp.float32) * s, 'Wk_up_e': jax.random.normal(ks[7], (L, DHE), jnp.float32) * s, 'Wv_up': jax.random.normal(ks[8], (L, DH), jnp.float32) * s, 'Wc': jax.random.normal(ks[9], (C, C), jnp.float32) * s}
    _L0_attn_in = _L0_attn_setup()

    def _L0_ffn_setup():
        import jax, jax.numpy as jnp
        import numpy as np
        D_MODEL = 256
        HIDDEN = 512
        N_EXPERTS = 8
        TOP_K = 2
        BATCH = 2
        SEQ = 512
        key = jax.random.key(seed)
        ks = jax.random.split(key, 9)
        s = 0.02
        return {'x': jax.random.normal(ks[0], (BATCH, SEQ, D_MODEL), dtype=jnp.float32), 'w_router': jax.random.normal(ks[1], (D_MODEL, N_EXPERTS), dtype=jnp.float32) * s, 'w1': jax.random.normal(ks[2], (N_EXPERTS, D_MODEL, HIDDEN), dtype=jnp.float32) * s, 'w3': jax.random.normal(ks[3], (N_EXPERTS, D_MODEL, HIDDEN), dtype=jnp.float32) * s, 'w2': jax.random.normal(ks[4], (N_EXPERTS, HIDDEN, D_MODEL), dtype=jnp.float32) * s, 'sw1': jax.random.normal(ks[5], (D_MODEL, HIDDEN), dtype=jnp.float32) * s, 'sw3': jax.random.normal(ks[6], (D_MODEL, HIDDEN), dtype=jnp.float32) * s, 'sw2': jax.random.normal(ks[7], (HIDDEN, D_MODEL), dtype=jnp.float32) * s}
    _L0_ffn_in = _L0_ffn_setup()
    _d = {'L0_attn_x': _L0_attn_in['x'], 'L0_attn_Wq_down': _L0_attn_in['Wq_down'], 'L0_attn_Wk_down': _L0_attn_in['Wk_down'], 'L0_attn_Wv_down': _L0_attn_in['Wv_down'], 'L0_attn_Wq_up_c': _L0_attn_in['Wq_up_c'], 'L0_attn_Wq_up_e': _L0_attn_in['Wq_up_e'], 'L0_attn_Wk_up_c': _L0_attn_in['Wk_up_c'], 'L0_attn_Wk_up_e': _L0_attn_in['Wk_up_e'], 'L0_attn_Wv_up': _L0_attn_in['Wv_up'], 'L0_attn_Wc': _L0_attn_in['Wc'], 'L0_ffn_w_router': _L0_ffn_in['w_router'], 'L0_ffn_w1': _L0_ffn_in['w1'], 'L0_ffn_w3': _L0_ffn_in['w3'], 'L0_ffn_w2': _L0_ffn_in['w2'], 'L0_ffn_sw1': _L0_ffn_in['sw1'], 'L0_ffn_sw3': _L0_ffn_in['sw3'], 'L0_ffn_sw2': _L0_ffn_in['sw2']}
    _x0 = _d['L0_attn_x']
    _d['L0_attn_x'] = jax.random.normal(jax.random.fold_in(jax.random.key(seed), 1), (4, 1024, 256), dtype=_x0.dtype)
    del _x0
    return _d

def reference(L0_attn_x, L0_attn_Wq_down, L0_attn_Wk_down, L0_attn_Wv_down, L0_attn_Wq_up_c, L0_attn_Wq_up_e, L0_attn_Wk_up_c, L0_attn_Wk_up_e, L0_attn_Wv_up, L0_attn_Wc, L0_ffn_w_router, L0_ffn_w1, L0_ffn_w3, L0_ffn_w2, L0_ffn_sw1, L0_ffn_sw3, L0_ffn_sw2):

    def _L0_attn_ref(x, Wq_down, Wk_down, Wv_down, Wq_up_c, Wq_up_e, Wk_up_c, Wk_up_e, Wv_up, Wc):
        import jax, jax.numpy as jnp
        import numpy as np
        import math
        B, T, C = (2, 512, 256)
        H, L = (16, 64)
        DH = C // H
        DHE = DH // 2
        THETA = 10000.0

        def _rope_cache(t, dim):
            inv_freq = 1.0 / THETA ** (jnp.arange(0, dim, 2, dtype=jnp.float32) / dim)
            freqs = jnp.arange(t, dtype=jnp.float32)[:, None] * inv_freq[None, :]
            emb = jnp.concatenate((freqs, freqs), axis=-1)
            return (jnp.cos(emb), jnp.sin(emb))

        def _apply_rope(x, cos, sin):
            x1 = x[..., 0::2]
            x2 = x[..., 1::2]
            rot = jnp.stack((-x2, x1), axis=-1).reshape(x.shape)
            return x * cos[None, None] + rot * sin[None, None]
        b, t, c = x.shape
        q_lat = (x @ Wq_down).reshape(b, t, H, L)
        k_lat = (x @ Wk_down).reshape(b, t, H, L)
        v_lat = (x @ Wv_down).reshape(b, t, H, L)
        q_c = jnp.einsum('bthl,ld->bhtd', q_lat, Wq_up_c)
        q_e = jnp.einsum('bthl,ld->bhtd', q_lat, Wq_up_e)
        k_c = jnp.einsum('bthl,ld->bhtd', k_lat, Wk_up_c)
        k_e = jnp.einsum('bthl,ld->bhtd', k_lat, Wk_up_e)
        v = jnp.einsum('bthl,ld->bhtd', v_lat, Wv_up)
        cos, sin = _rope_cache(t, DHE)
        q = jnp.concatenate([q_c, _apply_rope(q_e, cos, sin)], axis=-1)
        k = jnp.concatenate([k_c, _apply_rope(k_e, cos, sin)], axis=-1)
        scale = 1.0 / math.sqrt(DH)
        scores = jnp.einsum('bhqd,bhkd->bhqk', q, k) * scale
        causal = jnp.tril(jnp.ones((t, t), dtype=bool))
        scores = jnp.where(causal[None, None], scores, -jnp.inf)
        att = jax.nn.softmax(scores, axis=-1)
        y = jnp.einsum('bhqk,bhkd->bhqd', att, v)
        y = y.transpose(0, 2, 1, 3).reshape(b, t, c)
        return y @ Wc

    def _L0_ffn_ref(x, w_router, w1, w3, w2, sw1, sw3, sw2):
        import jax, jax.numpy as jnp
        import numpy as np
        D_MODEL = 256
        HIDDEN = 512
        N_EXPERTS = 8
        TOP_K = 2
        BATCH = 2
        SEQ = 512
        b, s, d = x.shape
        xf = x.reshape(b * s, d)
        probs = jax.nn.softmax(xf @ w_router, axis=-1)
        top_vals, top_idx = jax.lax.top_k(probs, TOP_K)
        gates = top_vals / jnp.sum(top_vals, axis=-1, keepdims=True)
        onehot = jax.nn.one_hot(top_idx, N_EXPERTS, dtype=xf.dtype)
        cw = jnp.einsum('tk,tke->te', gates, onehot)
        h1 = jnp.einsum('td,edh->eth', xf, w1)
        h3 = jnp.einsum('td,edh->eth', xf, w3)
        y = jnp.einsum('eth,ehd->etd', jax.nn.silu(h1) * h3, w2)
        out = jnp.einsum('etd,te->td', y, cw)
        out = out + jax.nn.silu(xf @ sw1) * (xf @ sw3) @ sw2
        return out.reshape(b, s, d)
    x = L0_attn_x
    x = x + 0.5 * _L0_ffn_ref(_layernorm(x, axis=-1), L0_ffn_w_router, L0_ffn_w1, L0_ffn_w3, L0_ffn_w2, L0_ffn_sw1, L0_ffn_sw3, L0_ffn_sw2)
    x = x + _L0_attn_ref(_layernorm(x, axis=-1), L0_attn_Wq_down, L0_attn_Wk_down, L0_attn_Wv_down, L0_attn_Wq_up_c, L0_attn_Wq_up_e, L0_attn_Wk_up_c, L0_attn_Wk_up_e, L0_attn_Wv_up, L0_attn_Wc)
    x = x + 0.5 * _L0_ffn_ref(_layernorm(x, axis=-1), L0_ffn_w_router, L0_ffn_w1, L0_ffn_w3, L0_ffn_w2, L0_ffn_sw1, L0_ffn_sw3, L0_ffn_sw2)
    return x

_drawn_inputs = setup_inputs


def setup_inputs(seed=0):
    import zlib

    import numpy as np

    out = dict(_drawn_inputs(seed))
    spreads = {}
    factors = {'L0_attn_Wq_down': 8.0,
     'L0_attn_Wk_down': 8.0,
     'L0_attn_Wv_down': 8.0,
     'L0_attn_Wq_up_c': 8.0,
     'L0_attn_Wq_up_e': 8.0,
     'L0_attn_Wk_up_c': 8.0,
     'L0_attn_Wk_up_e': 8.0,
     'L0_attn_Wv_up': 8.0,
     'L0_attn_Wc': 8.0,
     'L0_ffn_w_router': 3.856,
     'L0_ffn_w1': 3.36,
     'L0_ffn_w3': 3.329,
     'L0_ffn_w2': 3.327}
    for name, (base, spread) in spreads.items():
        noise = np.random.default_rng([zlib.crc32(name.encode()), seed]).standard_normal(out[name].shape)
        drawn = base * np.exp(spread * noise) if base else spread * noise
        out[name] = jnp.asarray(drawn.astype(out[name].dtype))
    for name, factor in factors.items():
        out[name] = (out[name] * factor).astype(out[name].dtype)
    return out
```

```python
from contextlib import ExitStack

import numpy as np
import concourse.bass as bass
from concourse import mybir

F32 = mybir.dt.float32
BF16 = mybir.dt.bfloat16
I32 = mybir.dt.int32
ALU = mybir.AluOpType
ACT = mybir.ActivationFunctionType
X = mybir.AxisListType.X

P = 128
B, S, D = 4, 1024, 256
T = B * S // P
KC = D // P
E, HID = 8, 512
HC = HID // P
ET = 2 * B * S // P + E
NT = T + ET
WE = 2 * KC * HID + HC * D
W3_AT, W2_AT = KC * HID, 2 * KC * HID
NH, DH, LAT = 16, 16, 64
EPS = 1e-5
THETA = 10000.0
NEG = -1.0e30
G4 = 4
NG = T // G4
NPART = 3
NPROD = 6
KQ = NPROD * DH
RING = 8
LEAD = 4
NHB = B * NH
QT = S // P


def host_constants():
    ident = np.eye(P, dtype=np.float32)
    k, m = np.arange(P)[:, None], np.arange(P)[None, :]
    prefix = np.stack([(k < m), np.ones((P, P), bool)], 1).astype(np.float32)
    route = np.zeros((P, E * T + E * T + E + ET), np.float32)
    route[:, :E * T] = np.tile((np.arange(T) > 0).astype(np.float32), E)
    route[:, E * T:2 * E * T] = np.tile(P * np.arange(T), E)
    route[:, 2 * E * T:2 * E * T + E] = E - np.arange(E)
    route[:, 2 * E * T + E:] = np.arange(ET)
    half = DH // 2
    inv = np.float32(1.0) / np.float32(THETA) ** (np.arange(0, half, 2, dtype=np.float32) / np.float32(half))
    freq = np.arange(S, dtype=np.float32)[:, None] * inv[None, :].astype(np.float32)
    emb = np.concatenate((freq, freq), -1)
    rope = np.stack([np.tile(np.cos(emb).T, (NH, 1)), np.tile(np.sin(emb).T, (NH, 1))], 1)
    mask = np.stack([np.where(m > k, NEG, 0.0), np.where(k > m, NEG, 0.0)], 1)
    return {"c_ident": ident, "c_prefix": prefix, "c_route": route,
            "c_rope": rope.astype(np.float32), "c_mask": mask.astype(np.float32)}


def build(nc, t, debug=None):
    ctx = ExitStack()
    with ctx:
        sb = lambda name, shape, dt=F32: ctx.enter_context(nc.sbuf_tensor(name, shape, dt))
        ps = lambda name, shape, dt=F32: ctx.enter_context(nc.psum_tensor(name, shape, dt))
        sem = lambda name: ctx.enter_context(nc.semaphore(name))
        dram = lambda name, shape, dt=F32: nc.dram_tensor(name, shape, dt)

        arena = sb("arena", [P, (E + 1) * WE])
        x_res = sb("x_res", [P, T, D])
        xnv = sb("xnv", [P, T, NH * (DH + 1)])
        xn_all = xnv[:, :, :].rearrange("p t c -> p (t c)")[:, 0:T * D].rearrange("p (t d) -> p t d", t=T)
        xin = sb("xin", [P, 2, D])
        xT = sb("xT", [P, 2, KC, P])
        sil_gat = sb("sil_gat", [P, 4, HID])
        sil, gat = sil_gat[:, 0:2, :], sil_gat[:, 2:4, :]
        yg = sil_gat[:, :, :].rearrange("p n (k d) -> p n k d", k=2)
        gT = sb("gT", [P, HC, P])
        prefix_f = gT[:, 0:2, :]
        ysb = sb("ysb", [P, 2, D])
        ident = sb("ident", [P, P])
        prefix_bf = sb("prefix_bf", [P, 2, P], BF16)
        route_c = sb("route_c", [P, 2 * E * T + E + ET])
        wr = sb("wr", [P, KC, E])
        stats = sb("stats", [P, T, 6])
        mv = sb("mv", [P, T, 2])
        rstd = sb("rstd", [P, T])
        vareps = sb("vareps", [P, T])
        mhalf = sb("mhalf", [P, T])
        in_gat = lambda i: gat[:, i // 2, (i % 2) * E * T:(i % 2 + 1) * E * T].rearrange("p (t e) -> p t e", e=E)
        prob, pick_a, tmp_a, tmp_b = (in_gat(i) for i in range(4))
        pick_b = sb("pick_b", [P, T, E])
        picks_bf = sb("picks_bf", [P, T, E], BF16)
        tot, incl = (ysb[:, i, :].rearrange("p (e t) -> p e t", e=E) for i in range(2))
        r_t = sb("r_t", [P, 6, T])
        r_e = sb("r_e", [P, 4, E])
        cmp_e = sb("cmp_e", [P, ET, E])
        te_f = sb("te_f", [P, ET])
        te_i = sb("te_i", [P, NT], I32)
        slot = sb("slot", [P, 2, T], I32)
        gates = sb("gates", [P, 2, T])

        room = {"at": WE}

        def in_arena(cols, dt=F32):
            a = arena[:, room["at"]:room["at"] + cols]
            room["at"] += cols
            assert room["at"] <= (E + 1) * WE
            return a if dt == F32 else a.bitcast(dt)

        w_qkv = in_arena(KC * 4 * D).rearrange("p (k c) -> p k c", k=KC)
        rope = in_arena(2 * S).rearrange("p (i t) -> p i t", i=2)
        xg = in_arena(G4 * D).rearrange("p (n d) -> p n d", n=G4)
        xgT = in_arena(2 * KC * G4 * P).rearrange("p (i k t) -> p i k t", i=2, k=KC)
        turn = in_arena(2 * 3 * G4 * P).rearrange("p (z i t) -> p z i t", z=2, i=3)
        rest = in_arena(4 * G4 * P).rearrange("p (z t) -> p z t", z=4)
        parts = in_arena(4 * 3 * G4 * P // 2, BF16).rearrange("p (z i t) -> p z i t", z=4, i=3)
        room["at"] = WE
        qst = in_arena(RING * S // 2, BF16).rearrange("p (n t) -> p n t", n=RING)
        kst = in_arena(RING * S // 2, BF16).rearrange("p (n t) -> p n t", n=RING)
        probs = [in_arena(S - P * u) for u in range(S // P)]
        y_all = in_arena(T * D).rearrange("p (b t h d) -> p b t h d", b=B, t=S // P, h=NH)
        mcol = in_arena(2 * 8).rearrange("p (i t) -> p i t", i=2)
        mrest = in_arena(P)
        m3 = in_arena(2 * 3 * P // 2, BF16).rearrange("p (i j t) -> p i j t", i=2, j=3)
        rden = in_arena(S // P)
        wc = gT[:, :, :].rearrange("p c t -> p (c t)").rearrange("p (k c) -> p k c", k=KC)
        vals = xnv[:, :, :].rearrange("p t c -> p (t c)").rearrange(
            "p (b g t h d) -> p b g t h d", b=B, g=2, t=S // P, h=NH // 2)
        ident_bf = sb("ident_bf", [P, P], BF16)
        mask_bf = sb("mask_bf", [P, 2, P], BF16)
        gstat = sb("gstat", [P, 8, G4])

        banks = ps("banks", [P, 8, 512])
        ps_h1, ps_h3 = banks[:, 0:2, :], banks[:, 2:4, :]
        ps_x, ps_y = banks[:, 4, :], banks[:, 6, :]
        ps_g = banks[:, 5, :].rearrange("p (c t) -> p c t", c=HC)
        ps_r = banks[:, 7, :].rearrange("p (i c) -> p i c", i=2)

        xs = dram("xs", [ET * P, D])
        ys = dram("ys", [ET * P, D])
        w_qkv_d = dram("w_qkv_d", [P, KC * 4 * D])
        qk_parts = [dram(f"{z}_parts", [B, NH, NPART, 2, DH // 2, S], BF16) for z in "qk"]

        s_const = sem("s_const")
        s_mask = sem("s_mask")
        s_masked = sem("s_masked")
        s_x = sem("s_x")
        s_w = sem("s_w")
        s_zero = sem("s_zero")
        s_zeroed = sem("s_zeroed")
        s_pool_c = sem("s_pool_c")
        s_prefix = sem("s_prefix")
        s_out = sem("s_out")
        A = {n: sem(f"a_{n}") for n in (
            "up0 up upload down wp wp_cp wp_st0 wp_st1 wload var sqrt xn tp xTc pv vc pqk chi ehi cmid emid t1 r1c t2 ep r1e "
            "loc_q loe_q loc_k loe_k st0 st1 st2 st3 ready "
            "ln0 ln1 nw smax rden ld0 ld1 mx s ed av norm mT m_hi m_parts m0 m1 ones wcl yld0 yld1 wtp wT wy wadd").split()}
        s_dve = sem("s_dve")
        dve_chain = [0]

        names = ("stat aggr vareps rstd xn kept r_tp r_xT r_lg smax expd picks rank routed pool_r sc_sh "
                 "xTp xTc h1 h3 sil g gt gTc y yS yE loaded0 loaded1 stored0 stored1 "
                 "gath0 gath1 gath2 gath3 comb0 comb")
        FS = [{n: sem(f"f{f}_{n}") for n in names.split()} for f in range(2)]

        def w_at(e, c, n):
            return arena[:, bass.ds(e + c, n)] if not isinstance(e, int) else arena[:, e + c:e + c + n]

        def need(eng, s, count):
            if not isinstance(count, int) or count > 0:
                eng.wait_ge(s, count)

        def steps(eng, first, last, body, peel_first=2, peel_last=2):
            for j in range(first, first + peel_first):
                body(j, j % 2)
            with eng.Fori(first + peel_first, last - peel_last - 1, 2) as j:
                body(j, 0)
                body(j + 1, 1)
            for j in range(last - peel_last, last):
                body(j, j % 2)


        def sp_ffn(sp, f):
            s = FS[f]

            def load(j, p, src):
                need(sp, s["xTp"], j - 1)
                sp.dma_start(xin[:, p, :], src).then_inc(s[f"loaded{p}"], 16)

            def load_shared(j, p):
                load(j, p, xn_all[:, bass.ds(j, 1) if not isinstance(j, int) else slice(j, j + 1), :]
                     .rearrange("p a d -> p (a d)"))

            def load_expert(j, p):
                load(j, p, xs[bass.ds(P * (j - T), P), :])

            def store(j, p):
                sp.wait_ge(s["yE"], j - T + 1)
                sp.dma_start(ys[bass.ds(P * (j - T), P), :], ysb[:, p, :]).then_inc(s[f"stored{p}"], 16)

            sp.wait_ge(s["r_tp"], T)
            sp.wait_ge(s["kept"], T)
            steps(sp, 0, T, load_shared)
            sp.wait_ge(s["sc_sh"], 2 * T * 16)

            def expert_step(j, p):
                if not isinstance(j, int) or j > T:
                    store(j - 1, 1 - p)
                load_expert(j, p)
            load_expert(T, 0)
            load_expert(T + 1, 1)
            with sp.Fori(T + 2, NT - 1, 2) as j:
                for p in range(2):
                    load_expert(j + p, p)
                    store(j + p - 2, p)
            store(NT - 2, 0)
            store(NT - 1, 1)

        def pool_ffn(pool, f):
            s = FS[f]
            pool.wait_ge(s["vareps"], 1)
            if f == 0:
                pool.wait_ge(s_pool_c, 1)
            nc.gpsimd.tensor_tensor(rstd[:, :], vareps[:, :], mhalf[:, :], ALU.pow).then_inc(s["rstd"], 1)

            def keep(j, p):
                pool.wait_ge(s["xn"], j + 1)
                dst = xn_all[:, bass.ds(j, 1), :] if not isinstance(j, int) else xn_all[:, j:j + 1, :]
                nc.gpsimd.tensor_copy(dst, xin[:, p:p + 1, :]).then_inc(s["kept"], 1)
            steps(pool, 0, T, keep, peel_last=0)
            pool.wait_ge(s["routed"], 1)
            pool.wait_ge(s["kept"], T)
            if f == 0:
                pool.wait_ge(s_zeroed, 16 * (ET // 8))
            for k in range(2):
                for i in range(T):
                    nc.gpsimd.indirect_dma_start(
                        out=xs[:, :], out_offset=bass.IndirectOffsetOnAxis(ap=slot[:, k, i:i + 1], axis=0),
                        in_=xn_all[:, i, :], in_offset=None).then_inc(s["sc_sh"], 16)

        def act_ffn(act, f):
            s = FS[f]

            def copy_xT(j, p, done, count, free, freed):
                act.wait_ge(done, count)
                need(act, free, freed)
                return nc.scalar.copy(xT[:, p, :, :].rearrange("p k t -> p (k t)"), ps_x[:, 0:D])

            steps(act, 0, T, lambda j, p: copy_xT(j, p, s["r_tp"], j + 1, s["r_lg"], j - 1)
                  .then_inc(s["r_xT"], 1), peel_last=0)
            act.wait_ge(s["smax"], 1)
            nc.scalar.activation(prob[:, :, :], tmp_a[:, :, :], ACT.Exp).then_inc(s["expd"], 1)
            act.wait_ge(s["expd"], 1)

            def xTc(j, p):
                if not isinstance(j, int) or j < NT:
                    copy_xT(j, p, s["xTp"], j + 1, s["h3"], j - 1).then_inc(s["xTc"], 1)

            def silu(j, p):
                if not isinstance(j, int) or j < NT:
                    act.wait_ge(s["h1"], j + 1)
                    need(act, s["g"], j - 1)
                    nc.scalar.activation(sil[:, p, :], ps_h1[:, p, :], ACT.Silu).then_inc(s["sil"], 1)

            def y_out(j, p):
                if isinstance(j, int) and j < T:
                    return
                act.wait_ge(s["y"], j + 1)
                if isinstance(j, int):
                    need(act, s[f"stored{p}"], 8 * (j - T - p))
                else:
                    act.wait_ge(s[f"stored{p}"], 8 * (j - T - p))
                nc.scalar.copy(ysb[:, p, :], ps_y[:, 0:D]).then_inc(s["yE"], 1)

            def step_shared(j, p):
                silu(j + 1, 1 - p)
                xTc(j + 2, p)

            def step_expert(j, p):
                silu(j + 1, 1 - p)
                xTc(j + 2, p)
                y_out(j, p)
            xTc(0, 0)
            xTc(1, 1)
            silu(0, 0)
            steps(act, 0, T, step_shared, peel_last=0)
            steps(act, T, NT, step_expert)

        def pe_transpose_rows(p):
            for k in range(KC):
                last = nc.tensor.transpose(ps_x[:, k * P:(k + 1) * P], xin[:, p, k * P:(k + 1) * P], ident[:, :])
            return last

        def pe_ffn(pe, f):
            s = FS[f]
            if f == 0:
                pe.wait_ge(s_const, N_CONST)
                pe.wait_ge(A["wp_cp"], 3 * KC)
            else:
                pe.wait_ge(A["wadd"], T)

            def rows(j, p):
                pe.wait_ge(s["xn"], j + 1)
                need(pe, s["r_xT"], j)
                pe_transpose_rows(p).then_inc(s["r_tp"], 1)

            def logits(j, p):
                pe.wait_ge(s["r_xT"], j + 1)
                at = ps_r[:, 0, bass.ds(E * j, E)]
                for k in range(KC):
                    last = nc.tensor.matmul(at, xT[:, p, k, :], wr[:, k, :], start=k == 0, stop=k == KC - 1)
                last.then_inc(s["r_lg"], 1)

            def router(j, p):
                if not isinstance(j, int) or j + 1 < T:
                    rows(j + 1, 1 - p)
                logits(j, p)
            rows(0, 0)
            steps(pe, 0, T, router)
            pe.wait_ge(s["picks"], 1)
            if f == 0:
                pe.wait_ge(s_prefix, 1)
            flat = picks_bf[:, :, :].rearrange("p t e -> p (t e)")
            for i in range(2):
                last = nc.tensor.matmul(ps_r[:, i, :], prefix_bf[:, i, :], flat, start=True, stop=True)
            last.then_inc(s["rank"], 1)

            def expert_of(j):
                if isinstance(j, int) and j < T:
                    return 0
                at = te_i[0:1, j:j + 1] if isinstance(j, int) else te_i[0:1, bass.ds(j, 1)]
                return pe.value_load(at, min_val=0, max_val=E * WE)

            def xTp(j, p):
                if not isinstance(j, int) or j < NT:
                    if isinstance(j, int):
                        pe.wait_ge(s[f"loaded{p}"], 8 * (j - p) + 16)
                    else:
                        pe.wait_ge(s[f"loaded{p}"], 8 * (j - p) + 16)
                    need(pe, s["xTc"], j)
                    pe_transpose_rows(p).then_inc(s["xTp"], 1)

            def hidden(j, p, e, out, at):
                for k in range(KC):
                    last = nc.tensor.matmul(out[:, p, :], xT[:, p, k, :], w_at(e, at + k * HID, HID),
                                            start=k == 0, stop=k == KC - 1)
                return last

            def h1(j, p, e):
                pe.wait_ge(s["xTc"], j + 1)
                need(pe, s["sil"], j - 1)
                hidden(j, p, e, ps_h1, 0).then_inc(s["h1"], 1)

            def h3(j, p, e):
                need(pe, s["g"], j - 1)
                hidden(j, p, e, ps_h3, W3_AT).then_inc(s["h3"], 1)

            def gt(j, p):
                pe.wait_ge(s["g"], j + 1)
                need(pe, s["gTc"], j)
                for c in range(HC):
                    last = nc.tensor.transpose(ps_g[:, c, :], gat[:, p, c * P:(c + 1) * P], ident[:, :])
                last.then_inc(s["gt"], 1)

            def y(j, p, e):
                pe.wait_ge(s["gTc"], j + 1)
                if isinstance(j, int):
                    if j <= T:
                        need(pe, s["yS"], j)
                    else:
                        need(pe, s["yE"], j - T)
                elif f_expert[0]:
                    pe.wait_ge(s["yE"], j - T)
                else:
                    pe.wait_ge(s["yS"], j)
                for c in range(HC):
                    last = nc.tensor.matmul(ps_y[:, 0:D], gT[:, c, :], w_at(e, W2_AT + c * D, D),
                                            start=c == 0, stop=c == HC - 1)
                last.then_inc(s["y"], 1)

            f_expert = [False]

            def tile(j, p):
                more = not isinstance(j, int) or j + 1 < NT
                e_next = expert_of_next(j + 1) if more else None
                if more:
                    h1(j + 1, 1 - p, e_next)
                gt(j, p)
                xTp(j + 2, p)
                if more:
                    h3(j + 1, 1 - p, e_next)
                y(j, p, expert_of(j) if f_expert[0] else 0)

            def expert_of_next(j):
                return expert_of(j) if (f_expert[0] or isinstance(j, int)) else 0

            pe.wait_ge(s_w, 16 * (N_W if f == 0 else 2 * N_W - 3))
            xTp(0, 0)
            xTp(1, 1)
            h1(0, 0, 0)
            h3(0, 0, 0)
            steps(pe, 0, T, tile)
            f_expert[0] = True
            steps(pe, T, NT, tile)

        def dve_ffn(dve, f):
            s = FS[f]

            def link(ins):
                dve_chain[0] += 1
                ins.then_inc(s_dve, 1)
                dve.wait_ge(s_dve, dve_chain[0])

            v = nc.vector
            if f == 0:
                dve.wait_ge(s_x, 16 * 4)
                dve.wait_ge(s_const, N_CONST)
                for i in range(2):
                    last = v.tensor_copy(prefix_bf[:, i, :], prefix_f[:, i, :])
                last.then_inc(s_prefix, 1)
                link(v.memset(te_i[:, 0:T], 0))
            with dve.Fori(0, T, 1) as i:
                v.bn_stats(stats[:, bass.ds(i, 1), :].rearrange("p a c -> p (a c)"),
                           x_res[:, bass.ds(i, 1), :].rearrange("p a c -> p (a c)")).then_inc(s["stat"], 1)
            dve.wait_ge(s["stat"], T)
            for i in range(T):
                v.bn_aggr(mv[:, i, :], stats[:, i, :]).then_inc(s["aggr"], 1)
            dve.wait_ge(s["aggr"], T)
            v.tensor_scalar(vareps[:, :], mv[:, :, 1], EPS, None, ALU.add).then_inc(s["vareps"], 1)

            def xn(j, p):
                need(dve, s["r_tp"], j - 1)
                need(dve, s["kept"], j - 1)
                at = slice(j, j + 1) if isinstance(j, int) else bass.ds(j, 1)
                v.tensor_scalar(xin[:, p, :], x_res[:, at, :].rearrange("p a c -> p (a c)"),
                                mv[:, at, 0], rstd[:, at], ALU.subtract, ALU.mult).then_inc(s["xn"], 1)
            dve.wait_ge(s["rstd"], 1)
            steps(dve, 0, T, xn, peel_last=0)

            dve.wait_ge(s["r_lg"], T)
            lg = ps_r[:, 0, :].rearrange("p (t e) -> p t e", e=E)
            over_e = lambda a: a.unsqueeze(2).to_broadcast([P, T, E])
            top, den, second = r_t[:, 0, :], r_t[:, 1, :], r_t[:, 2, :]
            link(v.tensor_reduce(top, lg, X, ALU.max))
            v.tensor_tensor(tmp_a[:, :, :], lg, over_e(top), ALU.subtract).then_inc(s["smax"], 1)
            dve.wait_ge(s["expd"], 1)
            link(v.tensor_reduce(den, prob[:, :, :], X, ALU.add))
            link(v.reciprocal(r_t[:, 3, :], den))
            link(v.tensor_tensor(prob[:, :, :], prob[:, :, :], over_e(r_t[:, 3, :]), ALU.mult))

            first_wins = route_c[:, 2 * E * T:2 * E * T + E].unsqueeze(1).to_broadcast([P, T, E])

            def pick(src, value, out):
                link(v.tensor_reduce(value, src, X, ALU.max))
                link(v.tensor_tensor(tmp_b[:, :, :], src, over_e(value), ALU.is_equal))
                link(v.tensor_tensor(tmp_b[:, :, :], tmp_b[:, :, :], first_wins, ALU.mult))
                link(v.tensor_reduce(r_t[:, 3, :], tmp_b[:, :, :], X, ALU.max))
                link(v.tensor_tensor(out, tmp_b[:, :, :], over_e(r_t[:, 3, :]), ALU.is_equal))
            pick(prob[:, :, :], top, pick_a[:, :, :])
            link(v.scalar_tensor_tensor(tmp_a[:, :, :], pick_a[:, :, :], -2.0, prob[:, :, :], ALU.mult, ALU.add))
            pick(tmp_a[:, :, :], second, pick_b[:, :, :])
            v.tensor_tensor(picks_bf[:, :, :], pick_a[:, :, :], pick_b[:, :, :], ALU.add).then_inc(s["picks"], 1)
            link(v.tensor_tensor(den, top, second, ALU.add))
            link(v.reciprocal(den, den))
            link(v.tensor_scalar(den, den, 0.5, None, ALU.mult))
            v.tensor_tensor(gates[:, 0, :], top, den, ALU.mult)
            link(v.tensor_tensor(gates[:, 1, :], second, den, ALU.mult))

            dve.wait_ge(s["rank"], 1)
            restart = route_c[:, 0:E * T]
            link(v.tensor_copy(tot[:, :, :], ps_r[:, 1, :].rearrange("p (t e) -> p e t", e=E)))
            flat = lambda a: a[:, :, :].rearrange("p e t -> p (e t)")
            link(v.tensor_tensor_scan(flat(incl), restart, flat(tot), 0.0, ALU.mult, ALU.add))
            over = tmp_a[:, :, :].rearrange("p t e -> p (t e)").rearrange("p (e t) -> p e t", e=E)
            thr = route_c[:, E * T:2 * E * T].rearrange("p (e t) -> p e t", e=E)
            link(v.tensor_tensor(over, incl[:, :, T - 1:T].to_broadcast([P, E, T]), thr, ALU.is_gt))
            n_tiles, end_tile, first_slot = r_e[:, 0, :], r_e[:, 1, :], r_e[:, 2, :]
            link(v.tensor_reduce(n_tiles, over, X, ALU.add))
            link(v.memset(r_e[:, 3, :], 1.0))
            link(v.tensor_tensor_scan(end_tile, r_e[:, 3, :], n_tiles, 0.0, ALU.mult, ALU.add))
            link(v.tensor_tensor(first_slot, end_tile, n_tiles, ALU.subtract))
            link(v.tensor_scalar(first_slot, first_slot, float(P), None, ALU.mult))
            link(v.tensor_tensor(incl[:, :, :], incl[:, :, :], tot[:, :, :], ALU.subtract))
            link(v.tensor_tensor(incl[:, :, :], incl[:, :, :], first_slot.unsqueeze(2).to_broadcast([P, E, T]), ALU.add))
            link(v.tensor_tensor(tmp_a[:, :, :], ps_r[:, 0, :].rearrange("p (t e) -> p t e", e=E),
                                 incl[:, :, :].rearrange("p e t -> p t e"), ALU.add))
            for k, picked in enumerate((pick_a, pick_b)):
                link(v.tensor_tensor(tmp_b[:, :, :], tmp_a[:, :, :], picked[:, :, :], ALU.mult))
                link(v.tensor_reduce(r_t[:, 4 + k, :], tmp_b[:, :, :], X, ALU.add))
                link(v.tensor_copy(slot[:, k, :], r_t[:, 4 + k, :]))
            link(v.tensor_tensor(cmp_e[:, :, :], end_tile.unsqueeze(1).to_broadcast([P, ET, E]),
                                 route_c[:, 2 * E * T + E:].unsqueeze(2).to_broadcast([P, ET, E]), ALU.is_le))
            link(v.tensor_reduce(te_f[:, :], cmp_e[:, :, :], X, ALU.add))
            link(v.tensor_scalar(te_f[:, :], te_f[:, :], float(E - 1), float(WE), ALU.min, ALU.mult))
            link(v.tensor_scalar(te_f[:, :], te_f[:, :], float(WE), None, ALU.add))
            v.tensor_copy(te_i[:, T:NT], te_f[:, :]).then_inc(s["routed"], 1)

            def g(j, p):
                if isinstance(j, int) and j >= NT:
                    return
                dve.wait_ge(s["sil"], j + 1)
                dve.wait_ge(s["h3"], j + 1)
                need(dve, s["gt"], j - 1)
                v.tensor_tensor(gat[:, p, :], ps_h3[:, p, :], sil[:, p, :], ALU.mult).then_inc(s["g"], 1)

            def gTc(j, p):
                dve.wait_ge(s["gt"], j + 1)
                need(dve, s["y"], j)
                v.tensor_copy(gT[:, :, :].rearrange("p c t -> p (c t)"),
                              ps_g[:, :, :].rearrange("p c t -> p (c t)")).then_inc(s["gTc"], 1)

            def y_add(j, p):
                dve.wait_ge(s["y"], j + 1)
                at = slice(j, j + 1) if isinstance(j, int) else bass.ds(j, 1)
                row = x_res[:, at, :].rearrange("p a c -> p (a c)")
                v.scalar_tensor_tensor(row, ps_y[:, 0:D], 0.5, row, ALU.mult, ALU.add).then_inc(s["yS"], 1)

            def step_shared(j, p):
                gTc(j, p)
                g(j + 1, 1 - p)
                y_add(j, p)

            def step_expert(j, p):
                gTc(j, p)
                g(j + 1, 1 - p)
            g(0, 0)
            steps(dve, 0, T, step_shared, peel_last=0)
            steps(dve, T, NT, step_expert)

        def pool_combine(pool, f):
            for p in range(2):
                pool.wait_ge(FS[f][f"stored{p}"], 16 * (ET // 2))
            for g in range(NG):
                gather_group(f, g)

        def dve_combine_tile(dve, f, i, p4, half):
            s, v = FS[f], nc.vector
            dve.wait_ge(s[f"gath{p4}"], half + 32)
            at = slice(i, i + 1) if isinstance(i, int) else bass.ds(i, 1)
            row = x_res[:, at, :].rearrange("p a c -> p (a c)")
            v.scalar_tensor_tensor(row, yg[:, p4, 0, :], gates[:, 0, at], row, ALU.mult, ALU.add)\
                .then_inc(s["comb0"], 1)
            dve.wait_ge(s["comb0"], i + 1)
            return v.scalar_tensor_tensor(row, yg[:, p4, 1, :], gates[:, 1, at], row, ALU.mult, ALU.add)\
                .then_inc(s["comb"], 1)

        NP = NH // 2
        flat_xnv = xnv[:, :, :].rearrange("p t c -> p (t c)")
        downT = flat_xnv[:, 2048:2048 + 3 * NP * D].rearrange("p (z n c) -> p z n c", z=3, n=NP)
        up_qk = sil_gat[:, 0, 0:2 * 3 * DH].rearrange("p (z i h d) -> p z i h d", z=2, i=3, h=2)
        up_v = sil_gat[:, 0, 2 * 3 * DH:2 * 3 * DH + 2 * DH].rearrange("p (h d) -> p h d", h=2)
        w_stage = sil_gat[:, 1:3, :]
        w_half = sil_gat[:, 1:4, :].rearrange("p n c -> p (n c)")
        QW = 3 * NH * DH // 2

        def sp_absorb(sp):
            for z, n in enumerate(("wq_dT", "wk_dT", "wv_dT")):
                sp.dma_start(downT[:, z, :, :], t[n].rearrange("(n p) c -> p n c", p=P)).then_inc(A["down"], 16)
            sp.wait_ge(A["up0"], 1)
            for h in range(2):
                rows = slice(LAT * h, LAT * (h + 1))
                for z, n in enumerate("qk"):
                    for i, m in enumerate("ce"):
                        sp.dma_start(up_qk[rows, z, i, h, :], t[f"w{n}_up_{m}"][:, :]).then_inc(A["upload"], 16)
                sp.dma_start(up_v[rows, h, :], t["wv_up"][:, :]).then_inc(A["upload"], 16)

        def pe_absorb(pe):
            pe.wait_ge(A["down"], 3 * 16)
            pe.wait_ge(A["up"], 1)
            for z in range(3):
                for k in range(KC):
                    u = up_v[:, :, :].rearrange("p h d -> p (h d)") if z == 2 else \
                        up_qk[:, z, :, :, :].rearrange("p i h d -> p (i h d)")
                    w = u.shape[1]
                    for n in range(NP):
                        last = nc.tensor.matmul(banks[:, 2 * z + k, n * w:(n + 1) * w],
                                                downT[:, z, n, k * P:(k + 1) * P], u, start=True, stop=True)
                    last.then_inc(A["wp"], 1)

        def act_absorb(act):
            for z in range(3):
                for k in range(KC):
                    i = 2 * z + k
                    act.wait_ge(A["wp"], i + 1)
                    if i >= 2:
                        act.wait_ge(A[f"wp_st{i % 2}"], 16 * (i // 2))
                    w = 2 * DH if z == 2 else 3 * DH
                    dst = w_half[:, (i % 2) * 768:(i % 2) * 768 + NP * w]
                    src = banks[:, i, 0:NP * w]
                    if z < 2:
                        dst = dst.rearrange("p (i n d) -> p n i d", i=3, n=NP)
                        src = src.rearrange("p (n i d) -> p n i d", n=NP, i=3)
                    nc.scalar.copy(dst, src).then_inc(A["wp_cp"], 1)
                    act.wait_ge(A["wp_cp"], i + 1)
                    act.dma_start(w_qkv_d[:, k * 4 * D + z * QW:k * 4 * D + z * QW + NP * w],
                                  w_half[:, (i % 2) * 768:(i % 2) * 768 + NP * w]).then_inc(A[f"wp_st{i % 2}"], 16)
            for i in range(2):
                act.wait_ge(A[f"wp_st{i}"], 16 * 3)


        def groups(eng, body):
            for g in range(2):
                body(g, g % 2, g // 2)
            with eng.Fori(2, NG - 3, 2) as g:
                body(g, 0, g // 2)
                body(g + 1, 1, g // 2)
            for g in range(NG - 2, NG):
                body(g, g % 2, g // 2)

        def more(g):
            return not isinstance(g, int) or g < NG

        def sp_project(sp):
            sp.wait_ge(FS[0]["y"], NT)
            sp.dma_start(w_qkv[:, :, :].rearrange("p k c -> p (k c)"), w_qkv_d[:, :]).then_inc(A["wload"], 16)
            sp.dma_start(rope[:, :, :], t["c_rope"][:, :, :]).then_inc(A["wload"], 16)

            def store(g, half, b):
                for z, n in enumerate(("q", "k")):
                    for ce in range(2):
                        sp.wait_ge(A[("loc_", "loe_")[ce] + n], g + 1)
                        for i in range(NPART):
                            dst = qk_parts[z][bass.ds(b, 1), :, i, ce, :, half * G4 * P:(half + 1) * G4 * P]
                            sp.dma_start(dst.rearrange("b h d t -> (b h) d t"), parts[:, 2 * z + ce, i, :])\
                                .then_inc(A[f"st{2 * z + ce}"], 16)
            groups(sp, store)

        def pool_project(pool):
            for p in range(2):
                pool.wait_ge(FS[0][f"stored{p}"], 16 * (ET // 2))
            gather_group(0, 0)
            for g in range(NG):
                if g + 1 < NG:
                    gather_group(0, g + 1)
                for z, n in enumerate("qk"):
                    for ce, m in enumerate(("c", "e")):
                        pool.wait_ge(A[m + "mid"], 2 * g + z + 1)
                        nc.gpsimd.tensor_tensor(parts[:, 2 * z + ce, 2, :], rest[:, 2 * z + ce, :],
                                                parts[:, 2 * z + ce, 1, :], ALU.subtract)\
                            .then_inc(A[("loc_", "loe_")[ce] + n], 1)

        def gather_group(f, g):
            s = FS[f]
            for i in range(G4 * g, G4 * (g + 1)):
                need(nc.gpsimd, s["comb"], i - G4 + 1)
                for k in range(2):
                    nc.gpsimd.indirect_dma_start(
                        out=yg[:, i % G4, k, :], out_offset=None, in_=ys[:, :],
                        in_offset=bass.IndirectOffsetOnAxis(ap=slot[:, k, i:i + 1], axis=0)
                    ).then_inc(s[f"gath{i % G4}"], 16)

        def act_project(act):
            def root(g):
                if more(g):
                    act.wait_ge(A["var"], g + 1)
                    nc.scalar.activation(gstat[:, 2, :], gstat[:, 1, :], ACT.Sqrt).then_inc(A["sqrt"], 1)

            def transposed(g, half):
                if more(g):
                    act.wait_ge(A["tp"], g + 1)
                    need(act, A["pqk"], 6 * (g - 1))
                    nc.scalar.copy(xgT[:, half, :, :], ps_h1[:, :, :]).then_inc(A["xTc"], 1)

            def head(z, ce, which, g):
                first = which == 0
                src = (ps_z(z, 0) if ce == 0 else turn[:, z, 2, :]) if first else rest[:, 2 * z + ce, :]
                nc.scalar.copy(parts[:, 2 * z + ce, which, :], src)\
                    .then_inc(A[("c", "e")[ce] + ("hi", "mid")[which]], 1)

            def body(g, half, b):
                root(g + 1)
                for i in range(2):
                    act.wait_ge(A["pv"], 2 * g + i + 1)
                    v4 = ps_h1[:, i, :].rearrange("p (t g h d) -> p g t h d", t=2, g=2, h=NH // 2)
                    for half_heads in range(2):
                        at = vals[:, bass.ds(b, 1), half_heads, 4 * half + 2 * i:4 * half + 2 * i + 2, :, 0:DH]
                        last = nc.scalar.copy(at.rearrange("p b t h d -> p (b t) h d"), v4[:, half_heads])
                    last.then_inc(A["vc"], 1)
                for z in range(2):
                    act.wait_ge(A["pqk"], 6 * g + 3 * z + 1)
                    need(act, A[f"st{2 * z}"], 48 * g)
                    head(z, 0, 0, g)
                    act.wait_ge(A["ep"], 2 * g + z + 1)
                    need(act, A[f"st{2 * z + 1}"], 48 * g)
                    head(z, 1, 0, g)
                    act.wait_ge(A["r1c"], 2 * g + z + 1)
                    head(z, 0, 1, g)
                    if z == 0:
                        transposed(g + 1, 1 - half)
                    act.wait_ge(A["r1e"], 2 * g + z + 1)
                    head(z, 1, 1, g)
            root(0)
            transposed(0, 0)
            groups(act, body)

        def ps_z(z, i):
            return banks[:, ((2, 3, 5), (4, 6, 7))[z][i], :]

        def pe_project(pe):
            def transpose(g):
                if more(g):
                    pe.wait_ge(A["xn"], G4 * (g + 1))
                    need(pe, A["vc"], 2 * g)
                    for k in range(KC):
                        for i in range(G4):
                            last = nc.tensor.transpose(ps_h1[:, k, i * P:(i + 1) * P],
                                                       xg[:, i, k * P:(k + 1) * P], ident[:, :])
                    last.then_inc(A["tp"], 1)

            def values(g, half):
                pe.wait_ge(A["xTc"], g + 1)
                for i in range(G4):
                    for k in range(KC):
                        last = nc.tensor.matmul(ps_h1[:, i // 2, (i % 2) * D:(i % 2 + 1) * D],
                                                xgT[:, half, k, i * P:(i + 1) * P],
                                                w_qkv[:, k, 2 * QW:2 * QW + D], start=k == 0, stop=k == KC - 1)
                    if i % 2:
                        last.then_inc(A["pv"], 1)

            def rows(g, half, z):
                for i in range(3):
                    if i == 0:
                        need(pe, A["r1c"], 2 * g - 1 + z)
                    else:
                        need(pe, A[f"t{i}"], 2 * g - 1 + z)
                    for k in range(KC):
                        at = z * QW + i * P
                        last = nc.tensor.matmul(ps_z(z, i), w_qkv[:, k, at:at + P],
                                                xgT[:, half, k, :], start=k == 0, stop=k == KC - 1)
                    last.then_inc(A["pqk"], 1)

            def body(g, half, b):
                values(g, half)
                rows(g, half, 0)
                transpose(g + 1)
                rows(g, half, 1)
            pe.wait_ge(A["wload"], 2 * 16)
            for n, count in (("sil", NT), ("g", NT), ("gTc", NT), ("xTc", NT), ("yE", ET)):
                pe.wait_ge(FS[0][n], count)
            transpose(0)
            groups(pe, body)

        def dve_project(dve):
            v = nc.vector
            s = FS[0]
            count = {"n": 0}

            def norm(g, half, b):
                if not more(g):
                    return
                for i in range(G4):
                    dve_combine_tile(dve, 0, G4 * g + i, i, 32 * g)
                dve.wait_ge(s["comb"], G4 * (g + 1))
                for i in range(G4):
                    at = bass.ds(G4 * g + i, 1)
                    v.bn_stats(stats[:, i, :], x_res[:, at, :].rearrange("p a c -> p (a c)")).then_inc(A["ln0"], 1)
                dve.wait_ge(A["ln0"], G4 * (g + 1))
                for i in range(G4):
                    v.bn_aggr(mv[:, i, :], stats[:, i, :]).then_inc(A["ln1"], 1)
                dve.wait_ge(A["ln1"], G4 * (g + 1))
                v.tensor_scalar(gstat[:, 1, :], mv[:, 0:G4, 1], EPS, None, ALU.add).then_inc(A["var"], 1)
                dve.wait_ge(A["sqrt"], g + 1)
                v.reciprocal(gstat[:, 3, :], gstat[:, 2, :]).then_inc(A["nw"], 1)
                dve.wait_ge(A["nw"], 5 * g + 1)
                v.tensor_tensor(gstat[:, 4, :], gstat[:, 3, :], gstat[:, 3, :], ALU.mult).then_inc(A["nw"], 1)
                dve.wait_ge(A["nw"], 5 * g + 2)
                v.tensor_tensor(gstat[:, 4, :], gstat[:, 4, :], gstat[:, 1, :], ALU.mult).then_inc(A["nw"], 1)
                dve.wait_ge(A["nw"], 5 * g + 3)
                v.tensor_scalar(gstat[:, 4, :], gstat[:, 4, :], -0.5, 1.5, ALU.mult, ALU.add).then_inc(A["nw"], 1)
                dve.wait_ge(A["nw"], 5 * g + 4)
                v.tensor_tensor(gstat[:, 5, :], gstat[:, 4, :], gstat[:, 3, :], ALU.mult).then_inc(A["nw"], 1)
                dve.wait_ge(A["nw"], 5 * g + 5)
                need(dve, A["tp"], g)
                for i in range(G4):
                    at = bass.ds(G4 * g + i, 1)
                    v.tensor_scalar(xg[:, i, :], x_res[:, at, :].rearrange("p a c -> p (a c)"),
                                    mv[:, i, 0:1], gstat[:, 5, i:i + 1], ALU.subtract, ALU.mult).then_inc(A["xn"], 1)

            def rotary(g, half, z, i):
                dve.wait_ge(A["pqk"], 6 * g + 3 * z + 2 + i)
                need(dve, A["ep"], 2 * (g - 1) + z + 1)
                v.tensor_tensor(turn[:, z, i, :], ps_z(z, 1 + i), rope[:, i, half * G4 * P:(half + 1) * G4 * P],
                                ALU.mult).then_inc(A[f"t{1 + i}"], 1)

            def summed(g, z):
                dve.wait_ge(A["t2"], 2 * g + z + 1)
                need(dve, A["r1e"], 2 * (g - 1) + z + 1)
                v.tensor_tensor(turn[:, z, 2, :], turn[:, z, 0, :], turn[:, z, 1, :], ALU.add).then_inc(A["ep"], 1)

            def remainder(g, z, ce):
                dve.wait_ge(A[("chi", "ehi")[ce]], 2 * g + z + 1)
                need(dve, A[("loc_", "loe_")[ce] + "qk"[z]], g)
                src = ps_z(z, 0) if ce == 0 else turn[:, z, 2, :]
                v.tensor_tensor(rest[:, 2 * z + ce, :], src, parts[:, 2 * z + ce, 0, :], ALU.subtract)\
                    .then_inc(A[("r1c", "r1e")[ce]], 1)

            def body(g, half, b):
                norm(g + 1, 1 - half, b)
                for z in range(2):
                    rotary(g, half, z, 0)
                    rotary(g, half, z, 1)
                    summed(g, z)
                    remainder(g, z, 0)
                    remainder(g, z, 1)
            dve.wait_ge(A["wload"], 2 * 16)
            norm(0, 0, 0)
            for g in range(NG):
                body(g, g % 2, g // 2)


        def heads(eng, body, ahead=LEAD):
            for n in range(2):
                body(n, n % 2)
            with eng.Fori(2, NHB - ahead - 1, 2) as n:
                body(n, 0)
                body(n + 1, 1)
            for n in range(NHB - ahead, NHB):
                body(n, n % 2)

        def one(x):
            return bass.ds(x, 1) if not isinstance(x, int) else slice(x, x + 1)

        LOADS = 16 * 9

        def sp_heads(sp):
            for z in range(4):
                sp.wait_ge(A[f"st{z}"], 48 * NG)
            sp.wait_ge(A["pqk"], 6 * NG)
            sp.wait_ge(A["pv"], 2 * NG)

            def stacks(n, p):
                if isinstance(n, int) and n >= NHB:
                    return
                need(sp, A["s"], QT * (n - RING + 1))
                need(sp, A[f"ld{p}"], LOADS * ((n - p) // 2))
                at = n % RING
                qh, kh = (z.rearrange("b h i c d t -> (b h) (i c d) t")[one(n)].rearrange("a r t -> (a r) t")
                          for z in (qk_parts[0][:], qk_parts[1][:]))
                row = 0
                for i, times in enumerate((3, 2, 1)):
                    n_rows = times * DH
                    for j in range(times):
                        dst = qst[row + j * DH:row + (j + 1) * DH, one(at), :].rearrange("p a t -> p (a t)")
                        sp.dma_start(dst, qh[i * DH:(i + 1) * DH, :]).then_inc(A[f"ld{p}"], 16)
                    dst = kst[row:row + n_rows, one(at), :].rearrange("p a t -> p (a t)")
                    sp.dma_start(dst, kh[0:n_rows, :]).then_inc(A[f"ld{p}"], 16)
                    row += n_rows

            def maxima(n, p):
                if isinstance(n, int) and n >= NHB:
                    return
                sp.wait_ge(A["m_parts"], n + 1)
                need(sp, A[f"m{p}"], 48 * ((n - p) // 2))
                for j in range(NPART):
                    dst = qst[KQ + j:KQ + j + 1, one(n % RING), :].rearrange("p a (q t) -> p (a q) t", q=QT)
                    sp.dma_start(dst, m3[0:QT, p, j, :])\
                        .then_inc(A[f"m{p}"], 16)

            def body(n, p):
                stacks(n + LEAD + 2, p)
                maxima(n + LEAD - 1, 1 - p)
            for n in range(LEAD + 2):
                stacks(n, n % 2)
            for n in range(LEAD - 1):
                maxima(n, n % 2)
            heads(sp, body, LEAD + 2)

        def act_heads(act):
            def body(n, p):
                for u in range(QT):
                    act.wait_ge(A["s"], QT * n + u + 1)
                    need(act, A["av"], QT * (n - 1) + u + 1)
                    nc.scalar.activation(probs[u][:, :], score(u)[:, 0:S - P * u], ACT.Exp,
                                         scale=DH ** -0.5).then_inc(A["ed"], 1)
            heads(act, body)

        def score(u):
            return banks[:, 2 + 2 * (u % 2):4 + 2 * (u % 2), :].rearrange("p i c -> p (i c)")

        def pieces(at, n):
            while n > 0:
                w = min(n, 512 - at % 512)
                yield at, w
                at, n = at + w, n - w

        ps_max = banks[:, 0:2, :].rearrange("p i c -> p (i c)")
        ps_av = banks[:, 6, 0:QT * (DH + 1)].rearrange("p (t d) -> p t d", t=QT)
        ps_mT = banks[:, 7, 0:P]

        def max_at(u):
            return 512 * (u % 2) if u < QT // 2 else 0

        def pe_heads(pe):
            def most(n, u):
                if isinstance(n, int) and n >= NHB:
                    return
                if u == 0:
                    pe.wait_ge(A[f"ld{head_p[0]}"], LOADS * ((n - head_p[0]) // 2) + LOADS)
                before = {0: 0, 1: 0, 2: 1, 3: 2}.get(u, u)
                need(pe, A["mx"], QT * n + before)
                slot_n = one(n % RING)
                at, width = max_at(u), P * (u + 1)
                q = qst[0:KQ, slot_n, u * P:(u + 1) * P].rearrange("p a t -> p (a t)")
                for c, w in pieces(at, width):
                    k = kst[0:KQ, slot_n, c - at:c - at + w].rearrange("p a t -> p (a t)")
                    end = c - at + w == width
                    nc.tensor.matmul(ps_max[:, c:c + w], q, k, start=True, stop=not end)
                last = nc.tensor.matmul(ps_max[:, at + width - P:at + width], ident_bf[:, :], mask_bf[:, 0, :],
                                        start=False, stop=True)
                last.then_inc(A["smax"], 1)

            def max_rows(n, p):
                if isinstance(n, int) and n >= NHB:
                    return
                pe.wait_ge(A["mx"], QT * (n + 1))
                need(pe, A["m_parts"], n)
                nc.tensor.transpose(ps_mT[0:QT, :], mcol[:, p, :], ident[:, :]).then_inc(A["mT"], 1)

            def scores(n, u, p):
                if u == 0:
                    pe.wait_ge(A[f"m{p}"], 48 * ((n - p) // 2) + 48)
                need(pe, A["ed"], QT * n + u - 1)
                slot_n = one(n % RING)
                k = kst[0:KQ + NPART, slot_n, u * P:(u + 1) * P].rearrange("p a t -> p (a t)")
                out = score(u)
                for i, (c, w) in enumerate(pieces(0, S - P * u)):
                    q = qst[0:KQ + NPART, slot_n, u * P + c:u * P + c + w].rearrange("p a t -> p (a t)")
                    last = nc.tensor.matmul(out[:, c:c + w], k, q, start=True, stop=i > 0)
                    if i == 0:
                        last = nc.tensor.matmul(out[:, 0:P], ident_bf[:, :], mask_bf[:, 1, :], start=False, stop=True)
                last.then_inc(A["s"], 1)

            def weighted(n, u):
                pe.wait_ge(A["ed"], QT * n + u + 1)
                if u == 0:
                    need(pe, A["norm"], n)
                b, g, h = n // NH, (n // (NH // 2)) % 2, n % (NH // 2)
                if isinstance(n, int):
                    v = vals[:, b, g, u, h, :]
                else:
                    flat = xnv[:, :, :].rearrange("p t c -> p (t c)")
                    v = flat[:, bass.ds((n // (NH // 2)) * (QT * (NH // 2) * (DH + 1))
                                        + (n % (NH // 2)) * (DH + 1) + u * (NH // 2) * (DH + 1), DH + 1)]
                for q in range(u, QT):
                    last = nc.tensor.matmul(ps_av[:, q, :], probs[u][:, (q - u) * P:(q - u + 1) * P], v,
                                            start=u == 0 and q == 0, stop=u == q, skip_group_check=True)
                last.then_inc(A["av"], 1)

            head_p = [0]

            def body(n, p):
                for u in range(QT):
                    head_p[0] = p
                    most(n + LEAD, u)
                    scores(n, u, p)
                    if u == 0:
                        if not isinstance(n, int) or n > 0:
                            weighted(n - 1, QT - 1)
                    else:
                        weighted(n, u - 1)
                    if u == 1:
                        max_rows(n + LEAD - 1, 1 - p)
            pe.wait_ge(A["ones"], 3)
            for n, count in (("vc", 2 * NG), ("r1c", 2 * NG), ("t1", 2 * NG), ("t2", 2 * NG)):
                pe.wait_ge(A[n], count)
            for n in range(LEAD):
                head_p[0] = n % 2
                for u in range(QT):
                    most(n, u)
                if n > 0:
                    max_rows(n - 1, 1 - n % 2)
            heads(pe, body)
            weighted(NHB - 1, QT - 1)

        def dve_heads(dve):
            v = nc.vector

            def most(n, p, u):
                if isinstance(n, int) and n >= NHB:
                    return
                dve.wait_ge(A["smax"], QT * n + u + 1)
                if u == 0:
                    need(dve, A["mT"], n - 1)
                at = max_at(u)
                v.tensor_reduce(mcol[:, p, u:u + 1], ps_max[:, at:at + P * (u + 1)], X, ALU.max, negate=True)\
                    .then_inc(A["mx"], 1)

            def max_parts(n, p):
                if isinstance(n, int) and n >= NHB:
                    return
                dve.wait_ge(A["mT"], n + 1)
                need(dve, A[f"m{p}"], 48 * ((n - p) // 2))
                m = [m3[0:QT, p, j, :] for j in range(NPART)]
                v.tensor_copy(m[0], ps_mT[0:QT, :]).then_inc(A["m_hi"], 1)
                dve.wait_ge(A["m_hi"], 3 * n + 1)
                v.tensor_tensor(mrest[0:QT, :], ps_mT[0:QT, :], m[0], ALU.subtract).then_inc(A["m_hi"], 1)
                dve.wait_ge(A["m_hi"], 3 * n + 2)
                v.tensor_copy(m[1], mrest[0:QT, :]).then_inc(A["m_hi"], 1)
                dve.wait_ge(A["m_hi"], 3 * n + 3)
                v.tensor_tensor(m[2], mrest[0:QT, :], m[1], ALU.subtract).then_inc(A["m_parts"], 1)

            def norm(n):
                dve.wait_ge(A["av"], QT * (n + 1))
                need(dve, A["norm"], n)
                v.reciprocal(rden[:, :], ps_av[:, :, DH:DH + 1].rearrange("p t a -> p (t a)")).then_inc(A["rden"], 1)
                dve.wait_ge(A["rden"], n + 1)
                dst = y_all.rearrange("p b t h d -> p b t (h d)")[:, one(n // NH), :, bass.ds(DH * (n % NH), DH)]\
                    .rearrange("p b t d -> p (b t) d")
                v.tensor_tensor(dst, ps_av[:, :, 0:DH], rden[:, :].unsqueeze(2).to_broadcast([P, QT, DH]), ALU.mult)\
                    .then_inc(A["norm"], 1)

            def body(n, p):
                for u in range(QT):
                    most(n + LEAD, p, u)
                    if u == 0 and (not isinstance(n, int) or n > 0):
                        norm(n - 1)
                    if u == 1:
                        max_parts(n + LEAD - 1, 1 - p)
            dve.wait_ge(A["pqk"], 6 * NG)
            dve.wait_ge(A["vc"], 2 * NG)
            dve.wait_ge(A["emid"], 2 * NG)
            for z in range(4):
                dve.wait_ge(A[f"st{z}"], 48 * NG)
            for n in ("loc_q", "loe_q", "loc_k", "loe_k"):
                dve.wait_ge(A[n], NG)
            v.memset(kst[KQ:KQ + NPART, :, :], 1.0).then_inc(A["ones"], 1)
            v.memset(vals.rearrange("p b g t h d -> p (b g t h) d")[:, :, DH:DH + 1], 1.0).then_inc(A["ones"], 1)
            v.tensor_copy(ident_bf[:, :], ident[:, :]).then_inc(A["ones"], 1)
            for n in range(LEAD):
                for u in range(QT):
                    most(n, n % 2, u)
                if n > 0:
                    max_parts(n - 1, 1 - n % 2)
            heads(dve, body)
            norm(NHB - 1)


        def sp_out(sp):
            sp.dma_start(wc, t["wc"].rearrange("(k p) c -> p k c", p=P)).then_inc(A["wcl"], 16)
            sp.wait_ge(A["norm"], NHB)
            rows = y_all.rearrange("p b t h d -> p (b t) (h d)")

            def load(j, p):
                need(sp, A["wtp"], j - 1)
                sp.dma_start(xin[:, p, :], rows[:, one(j), :].rearrange("p a c -> p (a c)")).then_inc(A[f"yld{p}"], 16)
            steps(sp, 0, T, load, peel_last=0)

        def act_out(act):
            def copy(j, p):
                act.wait_ge(A["wtp"], j + 1)
                need(act, A["wy"], j - 1)
                nc.scalar.copy(xT[:, p, :, :].rearrange("p k t -> p (k t)"), ps_x[:, 0:D]).then_inc(A["wT"], 1)
            steps(act, 0, T, copy, peel_last=0)

        def pe_out(pe):
            def rows(j, p):
                if isinstance(j, int) and j >= T:
                    return
                pe.wait_ge(A[f"yld{p}"], 8 * (j - p) + 16)
                need(pe, A["wT"], j)
                pe_transpose_rows(p).then_inc(A["wtp"], 1)

            def body(j, p):
                rows(j + 1, 1 - p)
                pe.wait_ge(A["wT"], j + 1)
                need(pe, A["wadd"], j)
                for k in range(KC):
                    last = nc.tensor.matmul(ps_y[:, 0:D], xT[:, p, k, :], wc[:, k, :], start=k == 0, stop=k == KC - 1)
                last.then_inc(A["wy"], 1)
            pe.wait_ge(A["wcl"], 16)
            for n, count in (("ed", QT * NHB), ("norm", NHB)):
                pe.wait_ge(A[n], count)
            rows(0, 0)
            steps(pe, 0, T, body)

        def dve_out(dve):
            def add(j, p):
                dve.wait_ge(A["wy"], j + 1)
                row = x_res[:, one(j), :].rearrange("p a c -> p (a c)")
                nc.vector.tensor_tensor(row, ps_y[:, 0:D], row, ALU.add).then_inc(A["wadd"], 1)
            steps(dve, 0, T, add, peel_last=0)
            dve.wait_ge(A["wadd"], T)

        N_CONST = 16 * 4
        N_W = 3 * (E + 1)

        block = ctx.enter_context(nc.Block())

        def load_experts(sp, first):
            for e in range(first, E + 1):
                for src, at, n in (("w1", 0, KC), ("w3", W3_AT, KC), ("w2", W2_AT, HC)):
                    w = t["s" + src] if e == 0 else t[src][e - 1]
                    width = w.shape[1]
                    at += e * WE
                    sp.dma_start(arena[:, at:at + n * width].rearrange("p (k h) -> p k h", k=n),
                                 w.rearrange("(k p) h -> p k h", p=P)).then_inc(s_w, 16)

        @block.sync
        def _(sp):
            xv = t["x"].rearrange("b (n p) d -> p (b n) d", p=P)
            ov = t["out"].rearrange("b (n p) d -> p (b n) d", p=P)
            for i in range(4):
                sp.dma_start(x_res[:, i * T // 4:(i + 1) * T // 4, :], xv[:, i * T // 4:(i + 1) * T // 4, :])\
                    .then_inc(s_x, 16)
            sp.dma_start(ident[:, :], t["c_ident"][:, :]).then_inc(s_const, 16)
            sp.dma_start(prefix_f[:, :, :], t["c_prefix"][:, :, :]).then_inc(s_const, 16)
            sp.dma_start(route_c[:, :], t["c_route"][:, :]).then_inc(s_const, 16)
            sp.dma_start(wr[:, :, :], t["w_router"].rearrange("(k p) e -> p k e", p=P)).then_inc(s_const, 16)
            sp_absorb(sp)
            sp.dma_start(gT[:, 2:4, :], t["c_mask"][:, :, :]).then_inc(s_mask, 16)
            load_experts(sp, 0)
            sp.wait_ge(s_zero, 1)
            zv = xs[:, :].rearrange("(n i p) d -> n p i d", p=P, i=8)
            for i in range(ET // 8):
                sp.dma_start(zv[i], xn_all[:, 0:8, :]).then_inc(s_zeroed, 16)
            sp_ffn(sp, 0)
            sp_project(sp)
            sp_heads(sp)
            sp_out(sp)
            sp.wait_ge(A["wtp"], T)
            load_experts(sp, 1)
            if debug != "attn":
                sp_ffn(sp, 1)
                for g in range(NG):
                    sp.wait_ge(FS[1]["comb"], G4 * (g + 1))
                    sp.dma_start(ov[:, G4 * g:G4 * (g + 1), :], x_res[:, G4 * g:G4 * (g + 1), :]).then_inc(s_out, 16)
                sp.wait_ge(s_out, 16 * NG)
            else:
                sp.wait_ge(A["wadd"], T)
                sp.dma_start(ov, x_res[:, :, :]).then_inc(s_out, 16)
                sp.wait_ge(s_out, 16)

        @block.gpsimd
        def _(pool):
            nc.gpsimd.memset(xn_all[:, 0:8, :], 0.0).then_inc(s_zero, 1)
            nc.gpsimd.memset(mhalf[:, :], -0.5).then_inc(s_pool_c, 1)
            pool.wait_ge(s_zeroed, 16 * (ET // 8))
            pool.wait_ge(A["wp"], 3 * KC)
            pool_ffn(pool, 0)
            pool_project(pool)
            if debug != "attn":
                pool_ffn(pool, 1)
                pool_combine(pool, 1)

        @block.scalar
        def _(act):
            act_absorb(act)
            act_ffn(act, 0)
            act_project(act)
            act_heads(act)
            act_out(act)
            if debug != "attn":
                act_ffn(act, 1)

        @block.tensor
        def _(pe):
            pe_absorb(pe)
            pe_ffn(pe, 0)
            pe_project(pe)
            pe_heads(pe)
            pe_out(pe)
            if debug != "attn":
                pe_ffn(pe, 1)

        @block.vector
        def _(dve):
            nc.vector.memset(sil_gat[:, 0, 0:2 * 3 * DH + 2 * DH], 0.0).then_inc(A["up0"], 1)
            dve.wait_ge(A["upload"], 10 * 16)
            for z in range(2):
                nc.vector.tensor_scalar(up_qk[:, z, 2, :, 0::2], up_qk[:, z, 1, :, 1::2], -1.0, None, ALU.mult)
                last = nc.vector.tensor_copy(up_qk[:, z, 2, :, 1::2], up_qk[:, z, 1, :, 0::2])
            last.then_inc(A["up"], 1)
            dve.wait_ge(s_mask, 16)
            nc.vector.tensor_copy(mask_bf[:, :, :], gT[:, 2:4, :]).then_inc(s_masked, 1)
            dve_ffn(dve, 0)
            dve_project(dve)
            dve_heads(dve)
            dve_out(dve)
            if debug != "attn":
                dve_ffn(dve, 1)
                with dve.Fori(0, T - G4 + 1, G4) as i:
                    for p in range(G4):
                        dve_combine_tile(dve, 1, i + p, p, 8 * i)


_NAMES = {"L0_attn_x": "x", "L0_ffn_w_router": "w_router", "L0_ffn_w1": "w1", "L0_ffn_w3": "w3", "L0_ffn_w2": "w2",
          "L0_ffn_sw1": "sw1", "L0_ffn_sw3": "sw3", "L0_ffn_sw2": "sw2", "L0_attn_Wq_up_c": "wq_up_c",
          "L0_attn_Wq_up_e": "wq_up_e", "L0_attn_Wk_up_c": "wk_up_c", "L0_attn_Wk_up_e": "wk_up_e",
          "L0_attn_Wv_up": "wv_up", "L0_attn_Wc": "wc"}
_TURNED = {"L0_attn_Wq_down": "wq_dT", "L0_attn_Wk_down": "wk_dT", "L0_attn_Wv_down": "wv_dT"}


def kernel(debug=None, **inputs):
    import concourse.bacc as bacc
    from concourse.bass_utils import run_bass_kernel_spmd

    nc = bacc.Bacc("TRN2", target_bir_lowering=False, num_devices=1)
    arrays = {short: np.ascontiguousarray(inputs[name]) for name, short in _NAMES.items()}
    arrays.update({short: np.ascontiguousarray(inputs[name].T) for name, short in _TURNED.items()})
    arrays.update(host_constants())
    t = {n: nc.dram_tensor(n, a.shape, mybir.dt.from_np(a.dtype), kind="ExternalInput").ap() for n, a in arrays.items()}
    t["out"] = nc.dram_tensor("out", (B, S, D), F32, kind="ExternalOutput").ap()
    build(nc, t, debug)
    r = run_bass_kernel_spmd(nc, [arrays], core_ids=[0])
    return r.results[0]["out"]
```

```python
from contextlib import ExitStack

import numpy as np
import concourse.bass as bass
from concourse import mybir

F32 = mybir.dt.float32
BF16 = mybir.dt.bfloat16
I32 = mybir.dt.int32
ALU = mybir.AluOpType
ACT = mybir.ActivationFunctionType
X = mybir.AxisListType.X

P = 128
B, S, D = 4, 1024, 256
T = B * S // P
KC = D // P
E, HID = 8, 512
HC = HID // P
QUAD = 32
ET = 2 * B * S // P + E
NT = T + ET
EARLY = 20
LATE = EARLY + ET
XQ = 4
TQ = T // XQ
COMBINED = 8
FIRST_W = 8
YG = 8
WE = 2 * KC * HID + HC * D
W3_AT, W2_AT = KC * HID, 2 * KC * HID
NH, DH, LAT = 16, 16, 64
EPS = 1e-5
THETA = 10000.0
NEG = -1.0e30
G4 = 4
NG = T // G4
NPART = 3
NPROD = 6
KQ = NPROD * DH
QT = S // P
BANK = 512
HQ = 4
NQ = B * NH // HQ
RING = 3
SUMS_COLS = 256
SCORE_COLS = 512
INVERT_AT = 16
MAX_AHEAD = 12


def host_constants():
    ident = np.eye(P, dtype=np.float32)
    k, m = np.arange(P)[:, None], np.arange(P)[None, :]
    prefix = np.stack([(k < m), np.ones((P, P), bool)], 1).astype(np.float32)
    route = np.zeros((P, E * T + E * T + E + ET + 1), np.float32)
    route[:, -1] = np.arange(P)
    route[:, :E * T] = np.tile((np.arange(T) > 0).astype(np.float32), E)
    route[:, E * T:2 * E * T] = np.tile(P * np.arange(T), E)
    route[:, 2 * E * T:2 * E * T + E] = E - np.arange(E)
    route[:, 2 * E * T + E:-1] = np.arange(ET)
    half = DH // 2
    inv = np.float32(1.0) / np.float32(THETA) ** (np.arange(0, half, 2, dtype=np.float32) / np.float32(half))
    freq = np.arange(S, dtype=np.float32)[:, None] * inv[None, :].astype(np.float32)
    emb = np.concatenate((freq, freq), -1)
    rope = np.stack([np.tile(np.cos(emb).T, (NH, 1)), np.tile(np.sin(emb).T, (NH, 1))], 1)
    mask = np.stack([np.where(m > k, NEG, 0.0), np.where(k > m, NEG, 0.0)], 1)
    return {"c_ident": ident, "c_prefix": prefix, "c_route": route,
            "c_rope": rope.astype(np.float32), "c_mask": mask.astype(np.float32)}


def build(nc, t):
    ctx = ExitStack()
    with ctx:
        sb = lambda name, shape, dt=F32: ctx.enter_context(nc.sbuf_tensor(name, shape, dt))
        ps = lambda name, shape, dt=F32: ctx.enter_context(nc.psum_tensor(name, shape, dt))
        sem = lambda name: ctx.enter_context(nc.semaphore(name))
        dram = lambda name, shape, dt=F32: nc.dram_tensor(name, shape, dt)

        arena = sb("arena", [P, (E + 1) * WE])
        x_res = sb("x_res", [P, T, D])
        xnv = sb("xnv", [P, T, D])
        xn_all = xnv
        xin = sb("xin", [P, 2, D])
        xT = sb("xT", [P, 2, KC, P])
        sil_gat = sb("sil_gat", [P, 4, HID])
        sil, gat = sil_gat[:, 0:2, :], sil_gat[:, 2:4, :]
        w_still = sb("w_still", [P, 2, KC * HID])
        free_before = w_still[:, :, :].rearrange("p i c -> p (i c)")
        prefix_f = free_before[:, 0:2 * P].rearrange("p (i t) -> p i t", i=2)
        mask_f = free_before[:, 2 * P:4 * P].rearrange("p (i t) -> p i t", i=2)
        zeros = free_before[:, 4 * P:4 * P + D]
        ysb = sb("ysb", [P, 2, D])
        ident = sb("ident", [P, P])
        prefix_bf = sb("prefix_bf", [P, 2, P], BF16)
        route_c = sb("route_c", [P, 2 * E * T + E + ET + 1])
        wr = sb("wr", [P, KC, QUAD])
        stats = sb("stats", [P, T, 6])
        mv = sb("mv", [P, T, 2])
        rstd = sb("rstd", [P, T])
        vareps = sb("vareps", [P, T])
        mhalf = sb("mhalf", [P, T])
        routing = sb("routing", [P, 4, E * T])
        prob, pick_a, tmp_a, tmp_b = (routing[:, i, :].rearrange("p (t e) -> p t e", e=E) for i in range(4))
        pick_b = sb("pick_b", [P, T, E])
        picks_bf = sb("picks_bf", [P, T, E], BF16)
        tot, incl = (ysb[:, i, :].rearrange("p (e t) -> p e t", e=E) for i in range(2))
        r_t = sb("r_t", [P, 6, T])
        r_e = sb("r_e", [P, 4, E])
        cmp_e = routing[:, :, :].rearrange("p i c -> p (i c)")[:, 0:ET * E].rearrange("p (t e) -> p t e", e=E)
        te_f = sb("te_f", [P, ET])
        te_i = sb("te_i", [P, NT], I32)
        slot = sb("slot", [P, 2, T], I32)
        pad_f = sb("pad_f", [P, 4, E])
        pad_slot = sb("pad_slot", [P, E], I32)
        gates = sb("gates", [P, 2, T])

        room = {"at": WE}

        def in_arena(cols, dt=F32):
            a = arena[:, room["at"]:room["at"] + cols]
            room["at"] += cols
            assert room["at"] <= (E + 1) * WE
            return a if dt == F32 else a.bitcast(dt)

        room["at"] = (E + 1) * WE - YG * 2 * D
        yg = in_arena(YG * 2 * D).rearrange("p (n k d) -> p n k d", n=YG, k=2)
        room["at"] = WE + 2 * HQ * S // 2
        w_qkv = in_arena(KC * 4 * D).rearrange("p (k c) -> p k c", k=KC)
        rope = in_arena(2 * S).rearrange("p (i t) -> p i t", i=2)
        xg = in_arena(G4 * D).rearrange("p (n d) -> p n d", n=G4)
        xgT = in_arena(2 * KC * G4 * P).rearrange("p (i k t) -> p i k t", i=2, k=KC)
        turn = in_arena(2 * 3 * G4 * P).rearrange("p (z i t) -> p z i t", z=2, i=3)
        rest = in_arena(4 * G4 * P).rearrange("p (z t) -> p z t", z=4)
        parts = in_arena(4 * 3 * G4 * P // 2, BF16).rearrange("p (z i t) -> p z i t", z=4, i=3)
        room["at"] = WE
        stacks_q_k = in_arena(RING * 2 * HQ * S // 2, BF16).rearrange("p (n z h t) -> p n z h t", n=RING, z=2, h=HQ)
        probs = in_arena(8 * S).rearrange("p (n t) -> p n t", n=8)
        vst = in_arena(HQ * QT * 2 * DH).rearrange("p (h t d) -> p h t d", h=HQ, t=QT)
        yraw = in_arena(S)
        mcol = in_arena(HQ * QT).rearrange("p (h t) -> p h t", h=HQ)
        mtail = in_arena(HQ * QT // 2).rearrange("p (h t) -> p h t", h=HQ)
        mfin = in_arena(HQ * QT)
        mrest = in_arena(P)
        den = in_arena(2 * QUAD).rearrange("p (i t) -> p i t", i=2)
        m3 = in_arena(3 * P // 2, BF16).rearrange("p (j t) -> p j t", j=3)
        room["at"] = WE + 2 * HQ * S // 2
        yT = in_arena(B * KC * S).rearrange("p (b k t) -> p b k t", b=B, k=KC)
        y_quad = sil_gat[0:HQ * DH, 0:2, :].rearrange("p n c -> p (n c)")
        r_quad = sil_gat[0:HQ * DH, 2:4, :].rearrange("p n c -> p (n c)")
        wc = free_before[:, 0:KC * D].rearrange("p (k c) -> p k c", k=KC)
        ident_bf = sb("ident_bf", [P, P], BF16)
        mask_bf = sb("mask_bf", [P, 2, P], BF16)
        gstat = sb("gstat", [P, 8, G4])

        xT4 = sil_gat[:, :, :].rearrange("p n c -> p (n c)").rearrange("p (n k t) -> p n k t", n=2, k=KC)
        lgT = [ysb[:, :, :].rearrange("p n c -> p (n c)"), xT[:, :, :, :].rearrange("p n k t -> p (n k t)")]

        banks = ps("banks", [P, 8, 512])
        ps_h1, ps_h3 = banks[:, 0:2, :], banks[:, 2:4, :]
        ps_x, ps_y = banks[:, 4, :], banks[:, 6, :]
        ps_r = banks[:, 7, :].rearrange("p (i c) -> p i c", i=2)

        xs = dram("xs", [ET * P, D])
        ys = dram("ys", [ET * P, D])
        w_qkv_d = dram("w_qkv_d", [P, KC * 4 * D])
        qk_parts = [dram(f"{z}_parts", [B, NH, NPART, 2, DH // 2, S], BF16) for z in "qk"]

        rden_d = dram("rden_d", [B * NH, S])
        yn_d = dram("yn_d", [B * NH * DH, S])
        y_raw_d = dram("y_raw_d", [B * NH * 2 * DH, S])

        s_const = sem("s_const")
        s_mask = sem("s_mask")
        s_x = [sem(f"s_x{i}") for i in range(XQ)]
        s_ws = sem("s_w_shared")
        s_w = sem("s_w_experts")
        s_zero = sem("s_zero")
        s_pads = sem("s_pads")
        s_prefix = sem("s_prefix")
        s_out = sem("s_out")
        A = {n: sem(f"a_{n}") for n in (
            "up0 up upload down wp wp_cp wp_st wload var sqrt xn tp xTc pv vc pqk chi ehi cmid emid t1 r1c t2 ep r1e "
            "loc_q loe_q loc_k loe_k st0 st1 st2 st3 "
            "ln0 ln1 nw ld smax mx mfin mT m_hi m_parts m ones vst1 vcp s ed av av0 yc0 yc1 ys0 ys1 "
            "wcl yld0 yld1 yld2 yld3 wy wadd dl dr ds nl nm ns").split()}
        s_dve = sem("s_dve")
        dve_chain = [0]

        names = ("stat aggr vareps rstd xn r_tp r_xT r_lg r_lc r_lt smax expd picks rank slots routed sc_sh "
                 "xTp xTc h1 h3 sil g w1s w3s y yS yE loaded0 loaded1 stored0 stored1 "
                 "comb0 comb")
        s_gath = [sem(f"s_gath{i}") for i in range(YG)]
        FS = [{n: sem(f"f{f}_{n}") for n in names.split()} for f in range(2)]

        def w_at(e, c, n):
            return arena[:, bass.ds(e + c, n)] if not isinstance(e, int) else arena[:, e + c:e + c + n]

        def one(x):
            return bass.ds(x, 1) if not isinstance(x, int) else slice(x, x + 1)

        def need(eng, s, count):
            if not isinstance(count, int) or count > 0:
                eng.wait_ge(s, count)

        def steps(eng, first, last, body, peel_first=2, peel_last=2):
            for j in range(first, first + peel_first):
                body(j, j % 2)
            with eng.Fori(first + peel_first, last - peel_last - 1, 2) as j:
                body(j, 0)
                body(j + 1, 1)
            for j in range(last - peel_last, last):
                body(j, j % 2)


        def load_projections(sp):
            sp.wait_ge(FS[0]["y"], LATE)
            sp.dma_start(w_qkv[:, :, :].rearrange("p k c -> p (k c)"), w_qkv_d[:, :]).then_inc(A["wload"], 16)
            sp.dma_start(rope[:, :, :], t["c_rope"][:, :, :]).then_inc(A["wload"], 16)

        def sp_ffn(sp, f):
            s = FS[f]

            def load(j, p, src):
                need(sp, s["xTp"], j - 1)
                sp.dma_start(xin[:, p, :], src).then_inc(s[f"loaded{p}"], 16)

            def load_shared(j, p):
                token = j if isinstance(j, int) and j < EARLY or shared_at[0] == 0 else j - ET
                if isinstance(j, int) and j < 2:
                    sp.wait_ge(s["xn"], token + 1)
                load(j, p, xn_all[:, one(token), :].rearrange("p a d -> p (a d)"))

            def load_expert(j, p):
                load(j, p, xs[bass.ds(P * (j - EARLY), P), :])

            def store(j, p):
                sp.wait_ge(s["yE"], j - EARLY + 1)
                sp.dma_start(ys[bass.ds(P * (j - EARLY), P), :], ysb[:, p, :]).then_inc(s[f"stored{p}"], 16)
            shared_at = [0]

            for j in range(3 * E - FIRST_W):
                load_shared(j, j % 2)
                load_experts(sp, [FIRST_W + j])
            steps(sp, 3 * E - FIRST_W, EARLY, load_shared, peel_first=0, peel_last=0)
            sp.wait_ge(s["sc_sh"], 2 * T * 16)
            if f == 0:
                sp.wait_ge(s_pads, 16 * E)
            for j in range(EARLY, EARLY + 3):
                load_expert(j, j % 2)
            with sp.Fori(EARLY + 3, LATE - 2, 2) as j:
                for i in range(2):
                    load_expert(j + i, 1 - i)
                    store(j + i - 3, i)
            load_expert(LATE - 1, 1)
            store(LATE - 4, 0)
            shared_at[0] = ET
            for j in range(LATE, LATE + 3):
                load_shared(j, j % 2)
                store(j - 3, 1 - j % 2)
            if f == 0:
                load_projections(sp)
            for j in range(LATE + 3, NT):
                load_shared(j, j % 2)

        def pool_ffn(pool, f):
            s = FS[f]
            if f == 0:
                pool.wait_ge(s_zero, 3)
            for q in range(XQ):
                pool.wait_ge(s["vareps"], q + 1)
                at = slice(q * TQ, (q + 1) * TQ)
                nc.gpsimd.tensor_tensor(rstd[:, at], vareps[:, at], mhalf[:, at], ALU.pow).then_inc(s["rstd"], 1)

            pool.wait_ge(s["slots"], 1)
            pool.wait_ge(s["xn"], T)
            for k in range(2):
                for i in range(T):
                    nc.gpsimd.indirect_dma_start(
                        out=xs[:, :], out_offset=bass.IndirectOffsetOnAxis(ap=slot[:, k, i:i + 1], axis=0),
                        in_=xn_all[:, i, :], in_offset=None).then_inc(s["sc_sh"], 16)
            if f == 0:
                pool.wait_ge(s["routed"], 1)
                for e in range(E):
                    nc.gpsimd.indirect_dma_start(
                        out=xs[:, :], out_offset=bass.IndirectOffsetOnAxis(ap=pad_slot[:, e:e + 1], axis=0),
                        in_=zeros, in_offset=None).then_inc(s_pads, 16)

        def act_ffn(act, f):
            s = FS[f]

            def copy_xT(j, p, done, count, free, freed):
                act.wait_ge(done, count)
                need(act, free, freed)
                return nc.scalar.copy(xT[:, p, :, :].rearrange("p k t -> p (k t)"), ps_x[:, 0:D])

            def logits_out(h):
                act.wait_ge(s["r_lg"], NG // 2 * (h + 1))
                nc.scalar.copy(lgT[h], banks[:, 4 + h, :]).then_inc(s["r_lc"], 1)

            for g in range(NG):
                act.wait_ge(s["r_tp"], g + 1)
                need(act, s["r_lg"], g - 1)
                nc.scalar.copy(xT4[:, g % 2, :, :], banks[:, 2 * (g % 2):2 * (g % 2) + 2, :]).then_inc(s["r_xT"], 1)
                if g == NG // 2 + 1:
                    logits_out(0)
            logits_out(1)

            def xTc(j, p):
                if not isinstance(j, int) or j < NT:
                    copy_xT(j, p, s["xTp"], j + 1, s["h3"], j - 1).then_inc(s["xTc"], 1)

            def silu(j, p):
                if not isinstance(j, int) or j < NT:
                    act.wait_ge(s["h1"], j + 1)
                    need(act, s["g"], j - 1)
                    nc.scalar.activation(sil[:, p, :], ps_h1[:, p, :], ACT.Silu).then_inc(s["sil"], 1)

            def y_out(j, p):
                act.wait_ge(s["y"], j + 1)
                need(act, s[f"stored{p}"], 8 * (j - EARLY - p))
                nc.scalar.copy(ysb[:, p, :], ps_y[:, 0:D]).then_inc(s["yE"], 1)

            def is_expert(j):
                return EARLY <= j < LATE if isinstance(j, int) else loop_of_experts[0]
            loop_of_experts = [False]

            def hold_still(j, i, at):
                act.wait_ge(s["h1"] if i == 0 else s["h3"], j)
                nc.scalar.copy(w_still[:, i, :], arena[:, bass.ds(at + i * W3_AT, KC * HID)])\
                    .then_inc(s["w1s" if i == 0 else "w3s"], 1)

            def step_shared(j, p):
                if isinstance(j, int) and j + 2 == EARLY:
                    act.wait_ge(s_w, 16 * 3 * E * (f + 1))
                    act.wait_ge(s["routed"], 1)
                    if f == 0:
                        act.wait_ge(s_pads, 16 * E)
                silu(j + 1, 1 - p)
                if is_expert(j + 2):
                    at = act.value_load(te_i[0:1, one(j + 2)], min_val=0, max_val=E * WE)
                    hold_still(j + 2, 0, at)
                xTc(j + 2, p)
                if is_expert(j + 2):
                    hold_still(j + 2, 1, at)

            def step_expert(j, p):
                step_shared(j, p)
                y_out(j, p)
            xTc(0, 0)
            xTc(1, 1)
            silu(0, 0)
            act.wait_ge(s["smax"], 1)
            nc.scalar.activation(prob[:, :, :], tmp_a[:, :, :], ACT.Exp).then_inc(s["expd"], 1)
            act.wait_ge(s["expd"], 1)
            steps(act, 0, EARLY, step_shared)
            loop_of_experts[0] = True
            steps(act, EARLY, LATE, step_expert)
            loop_of_experts[0] = False
            steps(act, LATE, NT, step_shared)

        def pe_transpose_rows(p):
            for k in range(KC):
                last = nc.tensor.transpose(ps_x[:, k * P:(k + 1) * P], xin[:, p, k * P:(k + 1) * P], ident[:, :])
            return last

        def pe_ffn(pe, f):
            s = FS[f]
            if f == 0:
                pe.wait_ge(s_const, N_CONST)
                pe.wait_ge(A["wp_cp"], 3 * KC)
            else:
                pe.wait_ge(A["wadd"], T // 2)

            def rows(g):
                pe.wait_ge(s["xn"], G4 * (g + 1))
                need(pe, s["r_xT"], g - 1)
                for k in range(KC):
                    for i in range(G4):
                        last = nc.tensor.transpose(banks[:, 2 * (g % 2) + k, i * P:(i + 1) * P],
                                                   xn_all[:, G4 * g + i, k * P:(k + 1) * P], ident[:, :])
                last.then_inc(s["r_tp"], 1)

            def logits(g):
                pe.wait_ge(s["r_xT"], g + 1)
                for k in range(KC):
                    for c in range(G4):
                        at = (g % (NG // 2)) * P
                        last = nc.tensor.matmul(banks[QUAD * c:QUAD * (c + 1), 4 + g // (NG // 2), at:at + P],
                                                wr[:, k, :], xT4[:, g % 2, k, c * P:(c + 1) * P],
                                                start=k == 0, stop=k == KC - 1, skip_group_check=True)
                last.then_inc(s["r_lg"], 1)

            def turned_logits(h):
                pe.wait_ge(s["r_lc"], h + 1)
                for i in range(NG // 2):
                    last = nc.tensor.transpose(banks[:, 6 + h, i * P:(i + 1) * P], lgT[h][:, i * P:(i + 1) * P],
                                               ident[:, :])
                last.then_inc(s["r_lt"], 1)

            rows(0)
            for g in range(NG):
                if g + 1 < NG:
                    rows(g + 1)
                logits(g)
                if g == NG // 2 + 2:
                    turned_logits(0)
            turned_logits(1)

            def ranks():
                pe.wait_ge(s["picks"], 1)
                if f == 0:
                    pe.wait_ge(s_prefix, 1)
                flat = picks_bf[:, :, :].rearrange("p t e -> p (t e)")
                for i in range(2):
                    last = nc.tensor.matmul(ps_r[:, i, :], prefix_bf[:, i, :], flat, start=True, stop=True)
                last.then_inc(s["rank"], 1)

            def is_expert(j):
                return EARLY <= j < LATE if isinstance(j, int) else loop_of_experts[0]
            loop_of_experts = [False]

            def weights_of(j):
                return pe.value_load(te_i[0:1, one(j)], min_val=0, max_val=E * WE) if is_expert(j) else 0

            def xTp(j, p):
                if not isinstance(j, int) or j < NT:
                    pe.wait_ge(s[f"loaded{p}"], 8 * (j - p) + 16)
                    need(pe, s["xTc"], j)
                    pe_transpose_rows(p).then_inc(s["xTp"], 1)

            def hidden(j, p, i, out):
                for c in range(HC):
                    for k in range(KC):
                        col = k * HID + c * P
                        w = w_still[:, i, col:col + P] if is_expert(j) else \
                            arena[:, i * W3_AT + col:i * W3_AT + col + P]
                        last = nc.tensor.matmul(out[:, p, c * P:(c + 1) * P], w, xT[:, p, k, :],
                                                start=k == 0, stop=k == KC - 1, skip_group_check=True)
                return last

            def h1(j, p):
                pe.wait_ge(s["xTc"], j + 1)
                need(pe, s["sil"], j - 1)
                if is_expert(j):
                    pe.wait_ge(s["w1s"], j - EARLY + 1)
                hidden(j, p, 0, ps_h1).then_inc(s["h1"], 1)

            def h3(j, p):
                need(pe, s["g"], j - 1)
                if is_expert(j):
                    pe.wait_ge(s["w3s"], j - EARLY + 1)
                hidden(j, p, 1, ps_h3).then_inc(s["h3"], 1)

            def y(j, p, e):
                pe.wait_ge(s["g"], j + 1)
                if isinstance(j, int) and j == 0:
                    pe.wait_ge(s["smax"], 1)
                before = j - 1 if isinstance(j, int) else j
                if is_expert(before):
                    pe.wait_ge(s["yE"], j - EARLY)
                else:
                    need(pe, s["yS"], j - ET if shared_late[0] else j)
                for c in range(HC):
                    last = nc.tensor.matmul(ps_y[:, 0:D], gat[:, p, c * P:(c + 1) * P], w_at(e, W2_AT + c * D, D),
                                            start=c == 0, stop=c == HC - 1)
                last.then_inc(s["y"], 1)

            shared_late = [False]

            def tile(j, p):
                if isinstance(j, int) and j + 1 == EARLY:
                    pe.wait_ge(s_w, 16 * 3 * E * (f + 1))
                    pe.wait_ge(s["routed"], 1)
                more = not isinstance(j, int) or j + 1 < NT
                if more:
                    h1(j + 1, 1 - p)
                xTp(j + 2, p)
                if more:
                    h3(j + 1, 1 - p)
                y(j, p, weights_of(j))

            if f == 0:
                pe.wait_ge(s_ws, 16 * 3)
            xTp(0, 0)
            xTp(1, 1)
            h1(0, 0)
            h3(0, 0)
            tile(0, 0)
            tile(1, 1)
            ranks()
            for j in range(2, 4):
                tile(j, j % 2)
            steps(pe, 4, EARLY, tile, peel_first=0)
            loop_of_experts[0] = True
            steps(pe, EARLY, LATE, tile)
            loop_of_experts[0], shared_late[0] = False, True
            steps(pe, LATE, NT, tile)

        def aggregate(dve, f, q):
            s, v = FS[f], nc.vector
            for i in range(q * TQ, (q + 1) * TQ):
                v.bn_aggr(mv[:, i, :], stats[:, i, :]).then_inc(s["aggr"], 1)
            dve.wait_ge(s["aggr"], TQ * (q + 1))
            at = slice(q * TQ, (q + 1) * TQ)
            v.tensor_scalar(vareps[:, at], mv[:, at, 1], EPS, None, ALU.add).then_inc(s["vareps"], 1)

        def normalise(dve, f, q):
            s, v = FS[f], nc.vector
            dve.wait_ge(s["rstd"], q + 1)
            if q == 0 and f == 0:
                dve.wait_ge(A["wp"], 3 * KC)
            elif q == 0:
                dve.wait_ge(A["vcp"], QT * NQ)
            for i in range(q * TQ, (q + 1) * TQ):
                v.tensor_scalar(xn_all[:, i, :], x_res[:, i, :], mv[:, i, 0:1], rstd[:, i:i + 1],
                                ALU.subtract, ALU.mult).then_inc(s["xn"], 1)

        def group_statistics(dve, g):
            if g >= NG:
                return
            s, v = FS[0], nc.vector
            for i in range(G4 * g, G4 * (g + 1)):
                if i >= COMBINED:
                    combine_tile(dve, 0, i)
            dve.wait_ge(s["comb"], G4 * (g + 1))
            for i in range(G4 * g, G4 * (g + 1)):
                v.bn_stats(stats[:, i, :], x_res[:, i, :]).then_inc(A["ln0"], 1)
            dve.wait_ge(A["ln0"], G4 * (g + 1))
            for i in range(G4 * g, G4 * (g + 1)):
                v.bn_aggr(mv[:, i, :], stats[:, i, :]).then_inc(A["ln1"], 1)
            dve.wait_ge(A["ln1"], G4 * (g + 1))
            need(dve, A["nw"], 5 * g)
            v.tensor_scalar(gstat[:, 1, :], mv[:, G4 * g:G4 * (g + 1), 1], EPS, None, ALU.add)\
                .then_inc(A["var"], 1)

        def group_rows(dve, g):
            if g >= NG:
                return
            v = nc.vector
            dve.wait_ge(A["sqrt"], g + 1)
            v.reciprocal(gstat[:, 3, :], gstat[:, 2, :]).then_inc(A["nw"], 1)
            dve.wait_ge(A["nw"], 5 * g + 1)
            v.tensor_tensor(gstat[:, 4, :], gstat[:, 3, :], gstat[:, 3, :], ALU.mult).then_inc(A["nw"], 1)
            dve.wait_ge(A["nw"], 5 * g + 2)
            v.tensor_tensor(gstat[:, 4, :], gstat[:, 4, :], gstat[:, 1, :], ALU.mult).then_inc(A["nw"], 1)
            dve.wait_ge(A["nw"], 5 * g + 3)
            v.tensor_scalar(gstat[:, 4, :], gstat[:, 4, :], -0.5, 1.5, ALU.mult, ALU.add).then_inc(A["nw"], 1)
            dve.wait_ge(A["nw"], 5 * g + 4)
            v.tensor_tensor(gstat[:, 5, :], gstat[:, 4, :], gstat[:, 3, :], ALU.mult).then_inc(A["nw"], 1)
            dve.wait_ge(A["nw"], 5 * g + 5)
            need(dve, A["tp"], g)
            for i in range(G4):
                at = G4 * g + i
                v.tensor_scalar(xg[:, i, :], x_res[:, at, :], mv[:, at, 0:1], gstat[:, 5, i:i + 1],
                                ALU.subtract, ALU.mult).then_inc(A["xn"], 1)

        def dve_ffn(dve, f):
            s = FS[f]

            def link(ins):
                dve_chain[0] += 1
                ins.then_inc(s_dve, 1)
                dve.wait_ge(s_dve, dve_chain[0])

            v = nc.vector
            if f == 0:
                dve.wait_ge(s_const, N_CONST)
                for i in range(2):
                    last = v.tensor_copy(prefix_bf[:, i, :], prefix_f[:, i, :])
                last.then_inc(s_prefix, 1)
                dve.wait_ge(s_mask, 16)
                v.tensor_copy(mask_bf[:, :, :], mask_f)
                link(v.memset(te_i[:, :], 0))
                for q in range(XQ):
                    dve.wait_ge(s_x[q], 16)
                    for i in range(q * TQ, (q + 1) * TQ):
                        v.bn_stats(stats[:, i, :], x_res[:, i, :]).then_inc(s["stat"], 1)
                    if q > 0:
                        normalise(dve, f, q - 1)
                    dve.wait_ge(s["stat"], TQ * (q + 1))
                    aggregate(dve, f, q)
            normalise(dve, f, XQ - 1)

            lg = banks[:, 6:8, :].rearrange("p h c -> p (h c)").rearrange("p (t e) -> p t e", e=QUAD)[:, :, 0:E]
            over_e = lambda a: a.unsqueeze(2).to_broadcast([P, T, E])
            top, den, second = r_t[:, 0, :], r_t[:, 1, :], r_t[:, 2, :]
            first_wins = route_c[:, 2 * E * T:2 * E * T + E].unsqueeze(1).to_broadcast([P, T, E])

            def pick(src, value, out):
                link(v.tensor_reduce(value, src, X, ALU.max))
                link(v.tensor_tensor(tmp_b[:, :, :], src, over_e(value), ALU.is_equal))
                link(v.tensor_tensor(tmp_b[:, :, :], tmp_b[:, :, :], first_wins, ALU.mult))
                link(v.tensor_reduce(r_t[:, 3, :], tmp_b[:, :, :], X, ALU.max))
                link(v.tensor_tensor(out, tmp_b[:, :, :], over_e(r_t[:, 3, :]), ALU.is_equal))
            def less_top():
                dve.wait_ge(s["r_lt"], 2)
                link(v.tensor_reduce(top, lg, X, ALU.max))
                v.tensor_tensor(tmp_a[:, :, :], lg, over_e(top), ALU.subtract).then_inc(s["smax"], 1)

            def softmax():
                dve.wait_ge(s["expd"], 1)
                link(v.tensor_reduce(den, prob[:, :, :], X, ALU.add))
                link(v.reciprocal(r_t[:, 3, :], den))
                link(v.tensor_tensor(prob[:, :, :], prob[:, :, :], over_e(r_t[:, 3, :]), ALU.mult))

            def first_pick():
                pick(prob[:, :, :], top, pick_a[:, :, :])

            def second_pick():
                link(v.scalar_tensor_tensor(tmp_a[:, :, :], pick_a[:, :, :], -2.0, prob[:, :, :], ALU.mult, ALU.add))
                pick(tmp_a[:, :, :], second, pick_b[:, :, :])
                v.tensor_tensor(picks_bf[:, :, :], pick_a[:, :, :], pick_b[:, :, :], ALU.add).then_inc(s["picks"], 1)

            def find_gates():
                link(v.tensor_tensor(den, top, second, ALU.add))
                link(v.reciprocal(den, den))
                link(v.tensor_scalar(den, den, 0.5, None, ALU.mult))
                v.tensor_tensor(gates[:, 0, :], top, den, ALU.mult)
                link(v.tensor_tensor(gates[:, 1, :], second, den, ALU.mult))

            n_tiles, end_tile, first_slot = r_e[:, 0, :], r_e[:, 1, :], r_e[:, 2, :]

            def rank_slots():
                dve.wait_ge(s["rank"], 1)
                restart = route_c[:, 0:E * T]
                link(v.tensor_copy(tot[:, :, :], ps_r[:, 1, :].rearrange("p (t e) -> p e t", e=E)))
                flat = lambda a: a[:, :, :].rearrange("p e t -> p (e t)")
                link(v.tensor_tensor_scan(flat(incl), restart, flat(tot), 0.0, ALU.mult, ALU.add))
                if f == 0:
                    link(v.tensor_copy(pad_f[:, 0, :], incl[:, :, T - 1]))
                over = tmp_a[:, :, :].rearrange("p t e -> p (t e)").rearrange("p (e t) -> p e t", e=E)
                thr = route_c[:, E * T:2 * E * T].rearrange("p (e t) -> p e t", e=E)
                link(v.tensor_tensor(over, incl[:, :, T - 1:T].to_broadcast([P, E, T]), thr, ALU.is_gt))
                link(v.tensor_reduce(n_tiles, over, X, ALU.add))
                link(v.memset(r_e[:, 3, :], 1.0))
                link(v.tensor_tensor_scan(end_tile, r_e[:, 3, :], n_tiles, 0.0, ALU.mult, ALU.add))
                link(v.tensor_tensor(first_slot, end_tile, n_tiles, ALU.subtract))
                link(v.tensor_scalar(first_slot, first_slot, float(P), None, ALU.mult))
                link(v.tensor_tensor(incl[:, :, :], incl[:, :, :], tot[:, :, :], ALU.subtract))
                link(v.tensor_tensor(incl[:, :, :], incl[:, :, :], first_slot.unsqueeze(2).to_broadcast([P, E, T]), ALU.add))
                link(v.tensor_tensor(tmp_a[:, :, :], ps_r[:, 0, :].rearrange("p (t e) -> p t e", e=E),
                                     incl[:, :, :].rearrange("p e t -> p t e"), ALU.add))

            def find_slots():
                for k, picked in enumerate((pick_a, pick_b)):
                    link(v.tensor_tensor(tmp_b[:, :, :], tmp_a[:, :, :], picked[:, :, :], ALU.mult))
                    link(v.tensor_reduce(r_t[:, 4 + k, :], tmp_b[:, :, :], X, ALU.add))
                    last = v.tensor_copy(slot[:, k, :], r_t[:, 4 + k, :])
                last.then_inc(s["slots"], 1)

            def pad_slots():
                lane = route_c[:, 2 * E * T + E + ET:]
                taken, own, left, before = (pad_f[:, i, :] for i in range(4))
                spare = r_e[:, 3, :]
                link(v.scalar_tensor_tensor(own, n_tiles, float(P), taken, ALU.mult, ALU.subtract))
                link(v.tensor_scalar(left, own, -1.0, float(P), ALU.mult, ALU.add))
                link(v.tensor_tensor_scan(before, spare, left, 0.0, ALU.mult, ALU.add))
                link(v.tensor_tensor(before, before, left, ALU.subtract))
                link(v.tensor_tensor(before, before, own, ALU.subtract))
                link(v.scalar_tensor_tensor(before, end_tile[:, E - 1:E].to_broadcast([P, E]), float(P), before,
                                            ALU.mult, ALU.add))
                link(v.tensor_tensor(taken, taken, first_slot, ALU.add))
                link(v.tensor_scalar(left, own, lane, None, ALU.is_gt))
                link(v.tensor_tensor(taken, taken, before, ALU.subtract))
                link(v.tensor_tensor(taken, taken, left, ALU.mult))
                link(v.tensor_tensor(taken, taken, before, ALU.add))
                link(v.tensor_scalar(taken, taken, lane, None, ALU.add))
                link(v.tensor_copy(pad_slot[:, :], taken))

            def tile_experts():
                link(v.tensor_tensor(cmp_e[:, :, :], end_tile.unsqueeze(1).to_broadcast([P, ET, E]),
                                     route_c[:, 2 * E * T + E:2 * E * T + E + ET].unsqueeze(2).to_broadcast([P, ET, E]), ALU.is_le))
                link(v.tensor_reduce(te_f[:, :], cmp_e[:, :, :], X, ALU.add))
                link(v.tensor_scalar(te_f[:, :], te_f[:, :], float(E - 1), float(WE), ALU.min, ALU.mult))
                link(v.tensor_scalar(te_f[:, :], te_f[:, :], float(WE), None, ALU.add))
                v.tensor_copy(te_i[:, EARLY:LATE], te_f[:, :]).then_inc(s["routed"], 1)

            def g(j, p):
                if isinstance(j, int) and j >= NT:
                    return
                dve.wait_ge(s["sil"], j + 1)
                dve.wait_ge(s["h3"], j + 1)
                need(dve, s["y"], j - 1)
                v.tensor_tensor(gat[:, p, :], ps_h3[:, p, :], sil[:, p, :], ALU.mult).then_inc(s["g"], 1)

            shared_late = [False]

            def y_add(j, p):
                dve.wait_ge(s["y"], j + 1)
                token = j - ET if shared_late[0] else j
                row = x_res[:, one(token), :].rearrange("p a c -> p (a c)")
                v.scalar_tensor_tensor(row, ps_y[:, 0:D], 0.5, row, ALU.mult, ALU.add).then_inc(s["yS"], 1)

            def step_shared(j, p):
                g(j + 1, 1 - p)
                y_add(j, p)

            def step_expert(j, p):
                g(j + 1, 1 - p)
            less_top()
            g(0, 0)
            softmax()
            step_shared(0, 0)
            first_pick()
            second_pick()
            step_shared(1, 1)
            find_gates()
            rank_slots()
            step_shared(2, 0)
            find_slots()
            step_shared(3, 1)
            if f == 0:
                pad_slots()
            tile_experts()
            steps(dve, 4, EARLY, step_shared, peel_first=0, peel_last=0)
            steps(dve, EARLY, LATE, step_expert, peel_last=0)
            shared_late[0] = True
            for j in range(LATE, NT):
                if f == 0 and j == NT - 1:
                    group_rows(dve, 0)
                step_shared(j, j % 2)
                if f == 0 and j == NT - COMBINED + G4:
                    group_statistics(dve, 0)
                if f == 1:
                    dve.wait_ge(s["yS"], j - ET + 1)
                    for i in range(gathered(j - LATE), gathered(j - LATE + 1)):
                        combine_tile(dve, f, i)
                if f == 0 and NT - COMBINED <= j:
                    combine_tile(dve, f, j - (NT - COMBINED))
                if f == 0 and LATE < j <= LATE + HQ:
                    v.memset(stacks_q_k[KQ:KQ + NPART, 0, KEYS, j - LATE - 1, :], 1.0).then_inc(A["ones"], 1)
            dve.wait_ge(s["yS"], T)
            if f == 1:
                for i in range(gathered(NT - LATE), T):
                    combine_tile(dve, f, i)

        def pool_combine(pool, f):
            for p in range(2):
                pool.wait_ge(FS[f][f"stored{p}"], 16 * (ET // 2))
            pool.wait_ge(FS[f]["y"], LATE)
            for g in range(NG):
                gather_group(f, g)

        def gathered(n):
            return min(max(0, 5 * (n - 2) // 2), T)

        def combine_tile(dve, f, i):
            s, v = FS[f], nc.vector
            dve.wait_ge(s_gath[i % YG], 32 * ((f * T + i) // YG + 1))
            at = slice(i, i + 1)
            row = x_res[:, i, :]
            v.scalar_tensor_tensor(row, yg[:, i % YG, 0, :], gates[:, 0, at], row, ALU.mult, ALU.add)\
                .then_inc(s["comb0"], 1)
            dve.wait_ge(s["comb0"], i + 1)
            return v.scalar_tensor_tensor(row, yg[:, i % YG, 1, :], gates[:, 1, at], row, ALU.mult, ALU.add)\
                .then_inc(s["comb"], 1)

        NP = NH // 2
        flat_xnv = xnv[:, :, :].rearrange("p t c -> p (t c)")
        downT = flat_xnv[:, 2048:2048 + 3 * NP * D].rearrange("p (z n c) -> p z n c", z=3, n=NP)
        room["at"] = (E + 1) * WE - 4 * DH * 2 - KC * 4 * D
        up_qk = in_arena(2 * 3 * DH).rearrange("p (z i h d) -> p z i h d", z=2, i=3, h=2)
        up_all = arena[:, room["at"] - 2 * 3 * DH:room["at"] + 2 * DH]
        up_v = in_arena(2 * DH).rearrange("p (h d) -> p h d", h=2)
        w_stage = in_arena(KC * 4 * D).rearrange("p (k c) -> p k c", k=KC)
        QW = 3 * NH * DH // 2

        def sp_absorb(sp):
            for z, n in enumerate(("wq_dT", "wk_dT", "wv_dT")):
                sp.dma_start(downT[:, z, :, :], t[n].rearrange("(n p) c -> p n c", p=P)).then_inc(A["down"], 16)
            sp.wait_ge(A["up0"], 1)
            for h in range(2):
                rows = slice(LAT * h, LAT * (h + 1))
                for z, n in enumerate("qk"):
                    for i, m in enumerate("ce"):
                        sp.dma_start(up_qk[rows, z, i, h, :], t[f"w{n}_up_{m}"][:, :]).then_inc(A["upload"], 16)
                sp.dma_start(up_v[rows, h, :], t["wv_up"][:, :]).then_inc(A["upload"], 16)

        def pe_absorb(pe):
            pe.wait_ge(A["down"], 3 * 16)
            pe.wait_ge(A["up"], 1)
            for z in range(3):
                for k in range(KC):
                    u = up_v[:, :, :].rearrange("p h d -> p (h d)") if z == 2 else \
                        up_qk[:, z, :, :, :].rearrange("p i h d -> p (i h d)")
                    w = u.shape[1]
                    for n in range(NP):
                        last = nc.tensor.matmul(banks[:, 2 * z + k, n * w:(n + 1) * w],
                                                downT[:, z, n, k * P:(k + 1) * P], u, start=True, stop=True)
                    last.then_inc(A["wp"], 1)

        def act_absorb(act):
            for z in range(3):
                for k in range(KC):
                    i = 2 * z + k
                    act.wait_ge(A["wp"], i + 1)
                    w = 2 * DH if z == 2 else 3 * DH
                    dst = w_stage[:, k, z * QW:z * QW + NP * w]
                    src = banks[:, i, 0:NP * w]
                    if z < 2:
                        dst = dst.rearrange("p (i n d) -> p n i d", i=3, n=NP)
                        src = src.rearrange("p (n i d) -> p n i d", n=NP, i=3)
                    nc.scalar.copy(dst, src).then_inc(A["wp_cp"], 1)


        def groups(eng, body):
            for g in range(2):
                body(g, g % 2, g // 2)
            with eng.Fori(2, NG - 3, 2) as g:
                body(g, 0, g // 2)
                body(g + 1, 1, g // 2)
            for g in range(NG - 2, NG):
                body(g, g % 2, g // 2)

        def more(g):
            return not isinstance(g, int) or g < NG

        def sp_project(sp):
            def store(g, half, b):
                if isinstance(g, int) and g == NG - 1:
                    for z in range(4):
                        sp.wait_ge(A[f"st{z}"], 48 * (NG - 1))
                    stacks(sp, 0)
                for z, n in enumerate(("q", "k")):
                    for ce in range(2):
                        sp.wait_ge(A[("loc_", "loe_")[ce] + n], g + 1)
                        for i in range(NPART):
                            dst = qk_parts[z][bass.ds(b, 1), :, i, ce, :, half * G4 * P:(half + 1) * G4 * P]
                            sp.dma_start(dst.rearrange("b h d t -> (b h) d t"), parts[:, 2 * z + ce, i, :])\
                                .then_inc(A[f"st{2 * z + ce}"], 16)
            groups(sp, store)

        def pool_project(pool):
            for p in range(2):
                pool.wait_ge(FS[0][f"stored{p}"], 16 * (ET // 2))
            pool.wait_ge(FS[0]["y"], LATE)
            for g in range(3):
                gather_group(0, g)
            for g in range(NG):
                for z, n in enumerate("qk"):
                    for ce, m in enumerate(("c", "e")):
                        pool.wait_ge(A[m + "mid"], 2 * g + z + 1)
                        nc.gpsimd.tensor_tensor(parts[:, 2 * z + ce, 2, :], rest[:, 2 * z + ce, :],
                                                parts[:, 2 * z + ce, 1, :], ALU.subtract)\
                            .then_inc(A[("loc_", "loe_")[ce] + n], 1)
                    if z == 0 and g + 3 < NG:
                        gather_group(0, g + 3)

        def gather_group(f, g):
            s = FS[f]
            for i in range(G4 * g, G4 * (g + 1)):
                need(nc.gpsimd, s["comb"], i - YG + 1)
                for k in range(2):
                    nc.gpsimd.indirect_dma_start(
                        out=yg[:, i % YG, k, :], out_offset=None, in_=ys[:, :],
                        in_offset=bass.IndirectOffsetOnAxis(ap=slot[:, k, i:i + 1], axis=0)
                    ).then_inc(s_gath[i % YG], 16)

        def act_project(act):
            def root(g):
                if more(g):
                    act.wait_ge(A["var"], g + 1)
                    nc.scalar.activation(gstat[:, 2, :], gstat[:, 1, :], ACT.Sqrt).then_inc(A["sqrt"], 1)

            def transposed(g, half):
                if more(g):
                    act.wait_ge(A["tp"], g + 1)
                    need(act, A["pqk"], 6 * (g - 1))
                    nc.scalar.copy(xgT[:, half, :, :], ps_h1[:, :, :]).then_inc(A["xTc"], 1)

            def head(z, ce, which, g):
                first = which == 0
                src = (ps_z(z, 0) if ce == 0 else turn[:, z, 2, :]) if first else rest[:, 2 * z + ce, :]
                nc.scalar.copy(parts[:, 2 * z + ce, which, :], src)\
                    .then_inc(A[("c", "e")[ce] + ("hi", "mid")[which]], 1)

            def body(g, half, b):
                for i in range(2):
                    act.wait_ge(A["pv"], 2 * g + i + 1)
                    nc.scalar.copy(flat_xnv[:, bass.ds((G4 * g + 2 * i) * D, 2 * D)], ps_h1[:, i, :])\
                        .then_inc(A["vc"], 1)
                for z in range(2):
                    act.wait_ge(A["pqk"], 6 * g + 3 * z + 1)
                    need(act, A[f"st{2 * z}"], 48 * g)
                    head(z, 0, 0, g)
                    act.wait_ge(A["ep"], 2 * g + z + 1)
                    need(act, A[f"st{2 * z + 1}"], 48 * g)
                    head(z, 1, 0, g)
                    act.wait_ge(A["r1c"], 2 * g + z + 1)
                    head(z, 0, 1, g)
                    if z == 0:
                        transposed(g + 1, 1 - half)
                        root(g + 2)
                    act.wait_ge(A["r1e"], 2 * g + z + 1)
                    head(z, 1, 1, g)
            root(0)
            transposed(0, 0)
            root(1)
            groups(act, body)

        def ps_z(z, i):
            return banks[:, ((2, 3, 5), (4, 6, 7))[z][i], :]

        def pe_project(pe):
            def transpose(g):
                if more(g):
                    pe.wait_ge(A["xn"], G4 * (g + 1))
                    need(pe, A["vc"], 2 * g)
                    for k in range(KC):
                        for i in range(G4):
                            last = nc.tensor.transpose(ps_h1[:, k, i * P:(i + 1) * P],
                                                       xg[:, i, k * P:(k + 1) * P], ident[:, :])
                    last.then_inc(A["tp"], 1)

            def values(g, half):
                pe.wait_ge(A["xTc"], g + 1)
                for i in range(G4):
                    for k in range(KC):
                        last = nc.tensor.matmul(ps_h1[:, i // 2, (i % 2) * D:(i % 2 + 1) * D],
                                                xgT[:, half, k, i * P:(i + 1) * P],
                                                w_qkv[:, k, 2 * QW:2 * QW + D], start=k == 0, stop=k == KC - 1)
                    if i % 2:
                        last.then_inc(A["pv"], 1)

            def rows(g, half, z):
                for i in range(3):
                    if i == 0:
                        need(pe, A["r1c"], 2 * g - 1 + z)
                    else:
                        need(pe, A[f"t{i}"], 2 * g - 1 + z)
                    for k in range(KC):
                        at = z * QW + i * P
                        last = nc.tensor.matmul(ps_z(z, i), w_qkv[:, k, at:at + P],
                                                xgT[:, half, k, :], start=k == 0, stop=k == KC - 1)
                    last.then_inc(A["pqk"], 1)

            def body(g, half, b):
                values(g, half)
                rows(g, half, 0)
                transpose(g + 1)
                rows(g, half, 1)
            pe.wait_ge(A["wload"], 2 * 16)
            for n, count in (("sil", NT), ("g", NT), ("xTc", NT), ("yE", ET), ("yS", T)):
                pe.wait_ge(FS[0][n], count)
            transpose(0)
            groups(pe, body)

        def dve_project(dve):
            v = nc.vector
            s = FS[0]
            count = {"n": 0}

            def rotary(g, half, z, i):
                dve.wait_ge(A["pqk"], 6 * g + 3 * z + 2 + i)
                need(dve, A["ep"], 2 * (g - 1) + z + 1)
                v.tensor_tensor(turn[:, z, i, :], ps_z(z, 1 + i), rope[:, i, half * G4 * P:(half + 1) * G4 * P],
                                ALU.mult).then_inc(A[f"t{1 + i}"], 1)

            def summed(g, z):
                dve.wait_ge(A["t2"], 2 * g + z + 1)
                need(dve, A["r1e"], 2 * (g - 1) + z + 1)
                v.tensor_tensor(turn[:, z, 2, :], turn[:, z, 0, :], turn[:, z, 1, :], ALU.add).then_inc(A["ep"], 1)

            def remainder(g, z, ce):
                dve.wait_ge(A[("chi", "ehi")[ce]], 2 * g + z + 1)
                need(dve, A[("loc_", "loe_")[ce] + "qk"[z]], g)
                src = ps_z(z, 0) if ce == 0 else turn[:, z, 2, :]
                v.tensor_tensor(rest[:, 2 * z + ce, :], src, parts[:, 2 * z + ce, 0, :], ALU.subtract)\
                    .then_inc(A[("r1c", "r1e")[ce]], 1)

            def body(g, half, b):
                group_rows(dve, g + 1)
                for z in range(2):
                    rotary(g, half, z, 0)
                    rotary(g, half, z, 1)
                    summed(g, z)
                    remainder(g, z, 0)
                    remainder(g, z, 1)
                    if z == 0:
                        group_statistics(dve, g + 2)
            group_statistics(dve, 1)
            v.tensor_copy(ident_bf[:, :], ident[:, :]).then_inc(A["ones"], 1)
            dve.wait_ge(A["wload"], 2 * 16)
            for g in range(NG):
                body(g, g % 2, g // 2)


        def quads(eng, body, ahead=2):
            body(0)
            with eng.Fori(1, NQ - ahead, 1) as quad:
                body(quad)
            for quad in range(NQ - ahead, NQ):
                body(quad)

        def exists(quad):
            return not isinstance(quad, int) or quad < NQ

        QUERIES, KEYS = 0, 1

        def stack_of(stack, n_rows, quad, h, at, n):
            return stacks_q_k[0:n_rows, one(quad % RING), stack, h, at:at + n].rearrange("p a t -> p (a t)")

        def max_chunks():
            for u in range(QT):
                for at in range(0, P * (u + 1), BANK):
                    n = min(P * (u + 1) - at, BANK)
                    together = min(BANK // n, HQ if u > 0 else HQ // 2)
                    for h in range(0, HQ, together):
                        yield u, at, n, range(h, h + together)
        MAX = list(max_chunks())
        NM = len(MAX)
        assert NM % 2 == 1

        def score_chunks():
            for u in range(QT):
                n = S - P * u
                together = min(2 * BANK // max(n, BANK // 2), HQ)
                for c in range(HQ // together):
                    yield u, c, n, range(c * together, (c + 1) * together), BANK if BANK // 2 < n <= BANK else n
        SCORE = list(score_chunks())
        NS = len(SCORE)
        assert NS % 2 == 0 and (NQ - 1) % RING == 0

        def scored(u):
            return sum(c[0] < u for c in SCORE)

        def score_pieces(i):
            u, c, n, hs, step = SCORE[i]
            return [(k, at, min(SCORE_COLS, n - at)) for k in range(len(hs)) for at in range(0, n, SCORE_COLS)]

        def quad_order():
            others = []
            for i, (u, c, n, hs, step) in enumerate(SCORE):
                for k, at, w in score_pieces(i):
                    others.append((("scores", i, k, at, w), w + (P if at == 0 else 0)))
                before = (u - 1) % QT
                chunks = sum(ch[0] == u for ch in SCORE)
                sums = [k for k in range(S // BANK) if (k + 1) * BANK > before * P]
                if c == min(1, chunks - 1) or (c == 2 and len(sums) > 1):
                    for k in sums if chunks < 4 else sums[c - 1:c]:
                        for q in range(max(k * BANK, before * P), (k + 1) * BANK, SUMS_COLS):
                            w = min(SUMS_COLS, (k + 1) * BANK - q)
                            others.append((("sums", before, q, w), HQ * w))
            total, at, m = sum(cost for _, cost in others), 0, 0
            for item, cost in others:
                yield item
                at += cost
                early = 1 if item[0] == "scores" and 0 < SCORE[item[1]][0] <= 3 and SCORE[item[1]][1] == 0 else 0
                while (m + 1) * total <= at * (NM + 1) + early * total and m < NM + 1:
                    yield "maxima", m
                    m += 1
            assert m == NM + 1
        ORDER = list(quad_order())

        def ahead_of(quad, m):
            m += MAX_AHEAD
            return quad + 1 + m // (NM + 1), m % (NM + 1)

        def maxima_before(do):
            for m in range(NM + 1 + MAX_AHEAD):
                do(m // (NM + 1), m % (NM + 1))

        ps_max = banks[:, 0:2, :]
        ps_av = banks[:, 6:8, :]

        def score(i):
            return banks[:, 2 + 2 * (i % 2):4 + 2 * (i % 2), :].rearrange("p i c -> p (i c)")

        LOADS = 16 * 9

        def stacks(sp, quad):
            if not exists(quad):
                return
            need(sp, A["s"], NS * (quad - RING + 1))
            need(sp, A["ld"], LOADS * quad)
            q_stack, k_stack = (stacks_q_k[:, one(quad % RING), z, :, :].rearrange("p a h t -> p (a h) t")
                                for z in (QUERIES, KEYS))
            q_rows, k_rows = (z[:].rearrange("b h i c d t -> (b h) (i c d) t")[bass.ds(HQ * quad, HQ)]
                              .rearrange("h r t -> r h t") for z in qk_parts)
            row = 0
            for i, times in enumerate((3, 2, 1)):
                n_rows = times * DH
                for j in range(times):
                    sp.dma_start(q_stack[row + j * DH:row + (j + 1) * DH],
                                 q_rows[i * DH:(i + 1) * DH]).then_inc(A["ld"], 16)
                sp.dma_start(k_stack[row:row + n_rows], k_rows[0:n_rows]).then_inc(A["ld"], 16)
                row += n_rows

        def results(sp, b):
            if b == 0:
                sp.wait_ge(A["s"], NS * (NQ - 1))
            sp.wait_ge(A["ns"], 16 * NQ // B * (b + 1))
            sp.dma_start(yT[:, b, :, :], yn_d[:, :].rearrange("(b k p) t -> b p k t", b=B, k=KC)[b])\
                .then_inc(A[f"yld{b}"], 16)

        def sp_heads(sp):
            for z in range(4):
                sp.wait_ge(A[f"st{z}"], 48 * NG)
            sp.wait_ge(A["pqk"], 6 * NG)
            sp.wait_ge(A["pv"], 2 * NG)

            def maxima(quad):
                if not exists(quad):
                    return
                sp.wait_ge(A["m_parts"], quad + 1)
                need(sp, A["m"], 48 * quad)
                for j in range(NPART):
                    dst = stacks_q_k[KQ + j:KQ + j + 1, one(quad % RING), QUERIES, :, :]\
                        .rearrange("p a h (q t) -> p (a h q) t", q=QT)
                    sp.dma_start(dst, m3[0:HQ * QT, j, :]).then_inc(A["m"], 16)

            def sums_out(quad, c):
                sp.wait_ge(A[f"yc{c}"], quad + 1)
                sp.dma_start(y_raw_d[bass.ds(P * quad, P), c * BANK:(c + 1) * BANK],
                             yraw[:, c * BANK:(c + 1) * BANK]).then_inc(A[f"ys{c}"], 16)

            def body(quad):
                if not isinstance(quad, int) or quad > 0:
                    sums_out(quad - 1, 1)
                if isinstance(quad, int) and quad == NQ - 1:
                    for b in range(B - 1):
                        results(sp, b)
                maxima(quad + 1)
                sums_out(quad, 0)
                stacks(sp, quad + RING)
            for quad in range(1, RING):
                stacks(sp, quad)
            sp.dma_start(wc, t["wc"].rearrange("(k p) c -> p k c", p=P)).then_inc(A["wcl"], 16)
            maxima(0)
            quads(sp, body, RING)
            sums_out(NQ - 1, 1)
            results(sp, B - 1)

        def pool_heads(pool):
            pool.wait_ge(A["pqk"], 6 * NG)
            pool.wait_ge(A["emid"], 2 * NG)
            for z in range(4):
                pool.wait_ge(A[f"st{z}"], 48 * NG)
            for n in ("loc_q", "loe_q", "loc_k", "loe_k"):
                pool.wait_ge(A[n], NG)
            nc.gpsimd.memset(vst[:, :, :, :], 1.0).then_inc(A["vst1"], 1)
            for n in range(1, RING):
                pool.wait_ge(A["vst1"], n)
                nc.gpsimd.memset(stacks_q_k[KQ:KQ + NPART, n, KEYS, :, :], 1.0).then_inc(A["vst1"], 1)
            pool.wait_ge(A["vst1"], RING)
            pool.wait_ge(A["vc"], 2 * NG)

            def denominators(quad):
                for c in range(2):
                    pool.wait_ge(A[f"ys{c}"], 16 * (quad + 1))
                need(pool, A["dr"], quad)
                src = y_raw_d[bass.ds(P * quad, P), :].rearrange("(h r) (a t) -> h r a t", h=HQ, t=QUAD)[:, DH]
                pool.dma_start(den[:, 0, :], src).then_inc(A["dl"], 16)

            def inverses(quad):
                pool.wait_ge(A["dr"], quad + 1)
                pool.dma_start(rden_d[bass.ds(HQ * quad, HQ), :].rearrange("h (a t) -> h a t", t=QUAD), den[:, 1, :])\
                    .then_inc(A["ds"], 16)

            def back(quad):
                pool.wait_ge(A["ds"], 16 * (quad + 1))
                need(pool, A["ns"], 16 * quad)
                pool.dma_start(y_quad, y_raw_d[bass.ds(P * quad, P), :].rearrange("(h r) t -> h r t", h=HQ)[:, 0:DH])\
                    .then_inc(A["nl"], 16)
                pool.dma_start(r_quad, rden_d[bass.ds(HQ * quad, HQ), :].unsqueeze(1).to_broadcast([HQ, DH, S]))\
                    .then_inc(A["nl"], 16)

            def normalise(quad):
                pool.wait_ge(A["nl"], 32 * (quad + 1))
                nc.gpsimd.tensor_tensor(y_quad, y_quad, r_quad, ALU.mult).then_inc(A["nm"], 1)
                pool.wait_ge(A["nm"], quad + 1)
                pool.dma_start(yn_d[bass.ds(HQ * DH * quad, HQ * DH), :], y_quad).then_inc(A["ns"], 16)

            after = {1: denominators, 3: inverses, 4: back, 6: normalise}

            def body(quad):
                for u in range(QT):
                    need(pool, A["av"], QT * (quad - 1) + u + 1)
                    v = flat_xnv[:, bass.ds(((quad // (NH // HQ)) * QT + u) * D + (quad % (NH // HQ)) * HQ * DH,
                                            HQ * DH)].rearrange("p (h d) -> p h d", h=HQ)
                    nc.gpsimd.tensor_copy(vst[:, :, u, 0:DH], v).then_inc(A["vcp"], 1)
                    if u in after and (not isinstance(quad, int) or quad > 0):
                        after[u](quad - 1)
            quads(pool, body, 0)
            for step in after.values():
                step(NQ - 1)

        def act_heads(act):
            def evacuate(quad, c):
                if c == 0:
                    act.wait_ge(A["av0"], quad + 1)
                else:
                    act.wait_ge(A["av"], QT * (quad + 1))
                need(act, A[f"ys{c}"], 16 * quad)
                nc.scalar.copy(yraw[:, c * BANK:(c + 1) * BANK], ps_av[:, c, :]).then_inc(A[f"yc{c}"], 1)

            def body(quad):
                for i, (u, c, n, hs, step) in enumerate(SCORE):
                    act.wait_ge(A["s"], NS * quad + i + 1)
                    if c == 0:
                        need(act, A["av"], QT * quad + u - 1)
                    at = lambda a: a[:, 0:len(hs) * step].rearrange("p (h t) -> p h t", t=step)[:, :, 0:n]
                    nc.scalar.activation(at(probs[:, 4 * (u % 2) + c, :]), at(score(i)), ACT.Exp,
                                         scale=DH ** -0.5).then_inc(A["ed"], 1)
                    if i == 1 and (not isinstance(quad, int) or quad > 0):
                        evacuate(quad - 1, 1)
                    if u == QT // 2 + 1 and c == 0:
                        evacuate(quad, 0)
            for z in range(4):
                act.wait_ge(A[f"st{z}"], 48 * NG)
            for n in ("loc_q", "loe_q", "loc_k", "loe_k"):
                act.wait_ge(A[n], NG)
            act.wait_ge(A["ep"], 2 * NG)
            act.wait_ge(FS[0]["comb"], T)
            quads(act, body, 0)
            evacuate(NQ - 1, 1)

        def pe_heads(pe):
            def maxima(quad, m):
                if not exists(quad):
                    return
                if m == NM:
                    pe.wait_ge(A["mfin"], 2 * quad + 2)
                    nc.tensor.transpose(ps_max[0:HQ * QT, m % 2, 0:P], mfin[:, :], ident[:, :]).then_inc(A["mT"], 1)
                    return
                u, at, n, hs = MAX[m]
                if m == 0:
                    pe.wait_ge(A["ld"], LOADS * (quad + 1))
                if m == 1:
                    need(pe, A["m_hi"], 3 * quad - 1)
                need(pe, A["mx"], NM * quad + max(m - 1, 0))
                bank = ps_max[:, m % 2, :]
                diagonal = at + n == P * (u + 1)
                for i, h in enumerate(hs):
                    last = nc.tensor.matmul(bank[:, i * n:(i + 1) * n], stack_of(QUERIES, KQ, quad, h, u * P, P),
                                            stack_of(KEYS, KQ, quad, h, at, n), start=True, stop=not diagonal,
                                            skip_group_check=True)
                    if diagonal:
                        last = nc.tensor.matmul(bank[:, (i + 1) * n - P:(i + 1) * n], ident_bf[:, :], mask_bf[:, 0, :],
                                                start=False, stop=True, skip_group_check=True)
                last.then_inc(A["smax"], 1)

            def scores(quad, i, k, at, w):
                u, c, n, hs, step = SCORE[i]
                if k == 0 and at == 0:
                    if i == 0:
                        pe.wait_ge(A["m"], 48 * (quad + 1))
                        if isinstance(quad, int) and quad == 0:
                            pe.wait_ge(A["vst1"], RING)
                    need(pe, A["ed"], NS * quad + i - 1)
                out = score(i)
                last = nc.tensor.matmul(out[:, k * step + at:k * step + at + w],
                                        stack_of(KEYS, KQ + NPART, quad, hs[k], u * P, P),
                                        stack_of(QUERIES, KQ + NPART, quad, hs[k], u * P + at, w),
                                        start=True, stop=at > 0, skip_group_check=True)
                if at == 0:
                    last = nc.tensor.matmul(out[:, k * step:k * step + P], ident_bf[:, :], mask_bf[:, 1, :],
                                            start=False, stop=True, skip_group_check=True)
                if (k, at, w) == score_pieces(i)[-1]:
                    last.then_inc(A["s"], 1)

            def sums(quad, u, q, w):
                c = q // BANK
                if q == max(u * P, c * BANK):
                    pe.wait_ge(A["vcp"], QT * quad + u + 1)
                    pe.wait_ge(A["ed"], NS * quad + scored(u + 1))
                    if u == 0:
                        need(pe, A[f"yc{c}"], quad)
                for h in range(HQ):
                    chunk, k, step = next((ch, hs.index(h), st) for (v, ch, n, hs, st) in SCORE if v == u and h in hs)
                    at = k * step + q - u * P
                    last = nc.tensor.matmul(ps_av[32 * h:32 * (h + 1), c, q - c * BANK:q - c * BANK + w],
                                            vst[:, h, u, :], probs[:, 4 * (u % 2) + chunk, at:at + w],
                                            start=u == 0 and q % BANK == 0, stop=u == (4 * (c + 1) - 1),
                                            skip_group_check=True)
                if q + w == S:
                    last.then_inc(A["av"], 1)
                elif q + w == BANK and u == QT // 2 - 1:
                    last.then_inc(A["av0"], 1)

            def body(quad):
                for what, *arg in ORDER:
                    if what == "scores":
                        scores(quad, *arg)
                    elif what == "maxima":
                        maxima(*ahead_of(quad, *arg))
                    elif arg[0] < QT - 1:
                        sums(quad, *arg)
                    elif not isinstance(quad, int) or quad > 0:
                        sums(quad - 1, *arg)
            pe.wait_ge(A["ones"], HQ + 1)
            pe.wait_ge(A["vc"], 2 * NG)
            maxima_before(maxima)
            for n in ("r1c", "t1", "t2"):
                pe.wait_ge(A[n], 2 * NG)
            quads(pe, body)
            sums(NQ - 1, QT - 1, S - P, P)

        def dve_heads(dve):
            v = nc.vector

            def finish(quad):
                dve.wait_ge(A["mx"], NM * (quad + 1))
                need(dve, A["mT"], quad)
                fin = mfin.rearrange("p (h t) -> p h t", h=HQ)
                v.tensor_copy(fin[:, :, 0:QT // 2], mcol[:, :, 0:QT // 2]).then_inc(A["mfin"], 1)
                v.tensor_tensor(fin[:, :, QT // 2:], mcol[:, :, QT // 2:], mtail[:, :, :], ALU.min)\
                    .then_inc(A["mfin"], 1)

            def parts_of(quad):
                src = ps_max[0:HQ * QT, NM % 2, 0:P]
                m = [m3[0:HQ * QT, j, :] for j in range(NPART)]
                dve.wait_ge(A["mT"], quad + 1)
                need(dve, A["m"], 48 * quad)
                v.tensor_copy(m[0], src).then_inc(A["m_hi"], 1)
                dve.wait_ge(A["m_hi"], 3 * quad + 1)
                v.tensor_tensor(mrest[0:HQ * QT, :], src, m[0], ALU.subtract).then_inc(A["m_hi"], 1)
                dve.wait_ge(A["m_hi"], 3 * quad + 2)
                v.tensor_copy(m[1], mrest[0:HQ * QT, :]).then_inc(A["m_hi"], 1)
                dve.wait_ge(A["m_hi"], 3 * quad + 3)
                v.tensor_tensor(m[2], mrest[0:HQ * QT, :], m[1], ALU.subtract).then_inc(A["m_parts"], 1)

            def maxima(quad, m):
                if not exists(quad):
                    return
                if m == NM:
                    finish(quad)
                    parts_of(quad)
                    return
                u, at, n, hs = MAX[m]
                dve.wait_ge(A["smax"], NM * quad + m + 1)
                if m == 0:
                    need(dve, A["mfin"], 2 * quad)
                dst = mtail[:, hs[0]:hs[-1] + 1, u - QT // 2:u - QT // 2 + 1] if at > 0 else \
                    mcol[:, hs[0]:hs[-1] + 1, u:u + 1]
                v.tensor_reduce(dst.rearrange("p h a -> p (h a)"),
                                ps_max[:, m % 2, 0:len(hs) * n].rearrange("p (h k) -> p h k", k=n),
                                X, ALU.max, negate=True).then_inc(A["mx"], 1)

            def invert(quad):
                dve.wait_ge(A["dl"], 16 * (quad + 1))
                need(dve, A["ds"], 16 * quad)
                v.reciprocal(den[:, 1, :], den[:, 0, :]).then_inc(A["dr"], 1)

            def body(quad):
                for m in range(NM + 1):
                    maxima(*ahead_of(quad, m))
                    if m == INVERT_AT and (not isinstance(quad, int) or quad > 0):
                        invert(quad - 1)
            dve.wait_ge(A["pqk"], 6 * NG)
            maxima_before(maxima)
            quads(dve, body)
            invert(NQ - 1)


        def dve_out(dve):
            v = nc.vector

            def add(i):
                dve.wait_ge(A["wy"], i + 1)
                row = x_res[:, 2 * i:2 * i + 2, :].rearrange("p a c -> p (a c)")
                v.tensor_tensor(row, banks[:, i % 4, :], row, ALU.add).then_inc(A["wadd"], 1)

            def statistics(i):
                dve.wait_ge(A["wadd"], i + 1)
                for k in range(2 * i, 2 * i + 2):
                    v.bn_stats(stats[:, k, :], x_res[:, k, :]).then_inc(FS[1]["stat"], 1)
            for i in range(T // 2 + 1):
                if i < T // 2:
                    add(i)
                if i > 0:
                    statistics(i - 1)
                if i > 0 and i % (TQ // 2) == 0:
                    q = i // (TQ // 2) - 1
                    dve.wait_ge(FS[1]["stat"], TQ * (q + 1))
                    aggregate(dve, 1, q)
                    if q > 0:
                        normalise(dve, 1, q - 1)

        def pe_out(pe):
            pe.wait_ge(A["wcl"], 16)
            pe.wait_ge(A["ed"], NS * NQ)
            pe.wait_ge(A["mx"], NM * NQ)
            for b in range(B):
                pe.wait_ge(A[f"yld{b}"], 16)
                for q in range(QT):
                    i = (QT * b + q) // 2
                    if q % 2 == 0:
                        need(pe, A["wadd"], i - 3)
                    for k in range(KC):
                        last = nc.tensor.matmul(banks[:, i % 4, (q % 2) * D:(q % 2 + 1) * D],
                                                yT[:, b, k, q * P:(q + 1) * P], wc[:, k, :],
                                                start=k == 0, stop=k == KC - 1, skip_group_check=True)
                    if q % 2:
                        last.then_inc(A["wy"], 1)

        N_CONST = 16 * 4

        block = ctx.enter_context(nc.Block())

        def load_weights(eng, e, i, signal):
            src, at, n = (("w1", 0, KC), ("w3", W3_AT, KC), ("w2", W2_AT, HC))[i]
            w = t["s" + src] if e == 0 else t[src][e - 1]
            width = w.shape[1]
            at += e * WE
            eng.dma_start(arena[:, at:at + n * width].rearrange("p (k h) -> p k h", k=n),
                          w.rearrange("(k p) h -> p k h", p=P)).then_inc(signal, 16)

        def load_experts(eng, which):
            for i in which:
                load_weights(eng, 1 + i // 3, i % 3, s_w)

        @block.sync
        def _(sp):
            xv = t["x"].rearrange("b (n p) d -> p (b n) d", p=P)
            ov = t["out"].rearrange("b (n p) d -> p (b n) d", p=P)
            sp_absorb(sp)
            sp.wait_ge(s_zero, 2)
            sp.dma_start(ident[:, :], t["c_ident"][:, :]).then_inc(s_const, 16)
            sp.dma_start(prefix_f[:, :, :], t["c_prefix"][:, :, :]).then_inc(s_const, 16)
            sp.dma_start(route_c[:, :], t["c_route"][:, :]).then_inc(s_const, 16)
            sp.dma_start(wr[:, :, 0:E], t["w_router"].rearrange("(k p) e -> p k e", p=P)).then_inc(s_const, 16)
            sp.dma_start(mask_f, t["c_mask"][:, :, :]).then_inc(s_mask, 16)
            for i in range(XQ):
                tiles = slice(i * T // XQ, (i + 1) * T // XQ)
                sp.dma_start(x_res[:, tiles, :], xv[:, tiles, :]).then_inc(s_x[i], 16)
            for i in range(3):
                load_weights(sp, 0, i, s_ws)
            sp.wait_ge(A["wp_cp"], 3 * KC)
            sp.dma_start(w_qkv_d[:, :], w_stage[:, :, :].rearrange("p k c -> p (k c)")).then_inc(A["wp_st"], 16)
            sp.wait_ge(A["wp_st"], 16)
            load_experts(sp, range(FIRST_W))
            sp_ffn(sp, 0)
            sp_project(sp)
            sp_heads(sp)
            sp.wait_ge(A["wy"], T // 2)
            load_experts(sp, range(FIRST_W))
            sp_ffn(sp, 1)
            for g in range(NG):
                sp.wait_ge(FS[1]["comb"], G4 * (g + 1))
                sp.dma_start(ov[:, G4 * g:G4 * (g + 1), :], x_res[:, G4 * g:G4 * (g + 1), :]).then_inc(s_out, 16)
            sp.wait_ge(s_out, 16 * NG)

        @block.gpsimd
        def _(pool):
            nc.gpsimd.memset(zeros, 0.0).then_inc(s_zero, 1)
            nc.gpsimd.memset(wr[:, :, :], 0.0).then_inc(s_zero, 1)
            nc.gpsimd.memset(mhalf[:, :], -0.5).then_inc(s_zero, 1)
            pool_ffn(pool, 0)
            pool_project(pool)
            pool_heads(pool)
            pool_ffn(pool, 1)
            pool_combine(pool, 1)

        @block.scalar
        def _(act):
            act_absorb(act)
            act_ffn(act, 0)
            act_project(act)
            act_heads(act)
            act_ffn(act, 1)

        @block.tensor
        def _(pe):
            pe_absorb(pe)
            pe_ffn(pe, 0)
            pe_project(pe)
            pe_heads(pe)
            pe_out(pe)
            pe_ffn(pe, 1)

        @block.vector
        def _(dve):
            nc.vector.memset(up_all, 0.0).then_inc(A["up0"], 1)
            dve.wait_ge(A["upload"], 10 * 16)
            for z in range(2):
                nc.vector.tensor_scalar(up_qk[:, z, 2, :, 0::2], up_qk[:, z, 1, :, 1::2], -1.0, None, ALU.mult)
                last = nc.vector.tensor_copy(up_qk[:, z, 2, :, 1::2], up_qk[:, z, 1, :, 0::2])
            last.then_inc(A["up"], 1)
            dve_ffn(dve, 0)
            dve_project(dve)
            dve_heads(dve)
            dve_out(dve)
            dve_ffn(dve, 1)

_NAMES = {"L0_attn_x": "x", "L0_ffn_w_router": "w_router", "L0_ffn_w1": "w1", "L0_ffn_w3": "w3", "L0_ffn_w2": "w2",
          "L0_ffn_sw1": "sw1", "L0_ffn_sw3": "sw3", "L0_ffn_sw2": "sw2", "L0_attn_Wq_up_c": "wq_up_c",
          "L0_attn_Wq_up_e": "wq_up_e", "L0_attn_Wk_up_c": "wk_up_c", "L0_attn_Wk_up_e": "wk_up_e",
          "L0_attn_Wv_up": "wv_up", "L0_attn_Wc": "wc"}
_TURNED = {"L0_attn_Wq_down": "wq_dT", "L0_attn_Wk_down": "wk_dT", "L0_attn_Wv_down": "wv_dT"}


def kernel(**inputs):
    import concourse.bacc as bacc
    from concourse.bass_utils import run_bass_kernel_spmd

    nc = bacc.Bacc("TRN2", target_bir_lowering=False, num_devices=1)
    arrays = {short: np.ascontiguousarray(inputs[name]) for name, short in _NAMES.items()}
    arrays.update({short: np.ascontiguousarray(inputs[name].T) for name, short in _TURNED.items()})
    arrays.update(host_constants())
    t = {n: nc.dram_tensor(n, a.shape, mybir.dt.from_np(a.dtype), kind="ExternalInput").ap() for n, a in arrays.items()}
    t["out"] = nc.dram_tensor("out", (B, S, D), F32, kind="ExternalOutput").ap()
    build(nc, t)
    r = run_bass_kernel_spmd(nc, [arrays], core_ids=[0])
    return r.results[0]["out"]
```
